# Optimizing a Trainium2 kernel written in Bass

```python
import numpy as np
import jax
import jax.numpy as jnp

def _softmax(x, axis=-1):
    return jax.nn.softmax(x, axis=axis)

def _gelu(x):
    return jax.nn.gelu(x, approximate=True)

def _silu(x):
    return jax.nn.silu(x)

def _sigmoid(x):
    return jax.nn.sigmoid(x)

def _layernorm(x, axis=-1, eps=1e-05):
    m = jnp.mean(x, axis=axis, keepdims=True)
    v = jnp.var(x, axis=axis, keepdims=True)
    return (x - m) / jnp.sqrt(v + eps)

def _scatter_add(tgt, idx, src, axis=0):
    return tgt.at[idx].add(src)

def _segment_sum(src, seg, n):
    return jax.ops.segment_sum(src, seg, n)
kernel_name = 'mk_perceiver_d1_seqx_r8_17d38c'

def setup_inputs(seed: int=0):
    np.random.seed(seed)
    _w = jnp.asarray

    def _rec_inputs():
        import jax
        import jax.numpy as jnp
        _rk = jax.random.key(seed)
        x = -0.0003929 + 0.9999 * jax.random.normal(jax.random.fold_in(_rk, 1), (16, 64, 256), jnp.float32)
        _lenS = 64 - jax.random.randint(jax.random.fold_in(_rk, 7), (16,), 0, max(1, 64 // 4) + 1, jnp.int32)
        _lenS2 = 1601 - jax.random.randint(jax.random.fold_in(_rk, 8), (16,), 0, max(1, 1601 // 4) + 1, jnp.int32)
        _ctx_1024P = jax.random.normal(jax.random.fold_in(_rk, 11), (16, 16, 128), jnp.float32)
        _ctx_1024c = jax.random.dirichlet(jax.random.fold_in(_rk, 511), 0.3 * jnp.ones((16,), jnp.float32), (16, 1601))
        _ctx_1024t = jnp.einsum('bsk,bkd->bsd', _ctx_1024c, _ctx_1024P)
        _ctx_1024t = _ctx_1024t * jax.lax.rsqrt(jnp.mean(jnp.square(_ctx_1024t)) + 1e-12) * 0.953939
        ctx_1024 = 0.000227908 + 0.99994 * (_ctx_1024t + 0.3 * jax.random.normal(jax.random.fold_in(_rk, 611), (16, 1601, 128), jnp.float32))
        return (x, ctx_1024)
    x, ctx_1024 = _rec_inputs()

    def _L0_xattn_setup():
        import jax, jax.numpy as jnp
        import numpy as np
        EPS = 1e-05

        def rmsnorm(x, g, eps=EPS):
            var = jnp.mean(jnp.square(x), axis=-1, keepdims=True)
            return x * jax.lax.rsqrt(var + eps) * g
        key = jax.random.key(seed)
        ks = jax.random.split(key, 8)
        B, Sq, Skv = (2, 512, 64)
        dim, cdim, H, D = (256, 128, 16, 128)
        inner = H * D
        s = lambda f: 1.0 / np.sqrt(f)
        return {'hidden_states': jax.random.normal(ks[0], (B, Sq, dim), jnp.float32), 'encoder_hidden_states': jax.random.normal(ks[1], (B, Skv, cdim), jnp.float32), 'Wq': jax.random.normal(ks[2], (dim, inner), jnp.float32) * s(dim), 'Wk': jax.random.normal(ks[3], (cdim, inner), jnp.float32) * s(cdim), 'Wv': jax.random.normal(ks[4], (cdim, inner), jnp.float32) * s(cdim), 'Wo': jax.random.normal(ks[5], (inner, dim), jnp.float32) * s(inner), 'gq': jnp.ones((D,), jnp.float32), 'gk': jnp.ones((D,), jnp.float32)}
    _L0_xattn_all = _L0_xattn_setup()
    _L0_xattn_in = {k: v for k, v in _L0_xattn_all.items() if k in ('Wq', 'Wk', 'Wv', 'Wo', 'gq', 'gk')}
    del _L0_xattn_all

    def _L0_attn_setup():
        import jax, jax.numpy as jnp
        import numpy as np
        FP8_MAX = 448.0
        NUM_HEADS = 16

        def act_quant(x):
            scale = jnp.max(jnp.abs(x)) / FP8_MAX
            q = (x / scale).astype(jnp.float8_e4m3fn)
            return (q, scale)
        key = jax.random.key(seed)
        k1, k2, k3, k4 = jax.random.split(key, 4)
        B, S, H = (2, 256, 256)
        x = jax.random.normal(k1, (B, S, H), dtype=jnp.float32)
        W_qkv = jax.random.normal(k2, (H, 3 * H), dtype=jnp.float32) * (1.0 / np.sqrt(H))
        W_out = jax.random.normal(k3, (H, H), dtype=jnp.float32) * (1.0 / np.sqrt(H))
        b_out = jnp.zeros((H,), dtype=jnp.float32)
        return {'x': x, 'W_qkv': W_qkv, 'W_out': W_out, 'b_out': b_out}
    _L0_attn_all = _L0_attn_setup()
    _L0_attn_in = {k: v for k, v in _L0_attn_all.items() if k in ('W_qkv', 'W_out', 'b_out')}
    del _L0_attn_all

    def _L0_ffn_setup():
        import jax, jax.numpy as jnp
        import numpy as np
        import math
        N_EMBD = 256
        N_HEAD = 16
        HEAD_DIM = N_EMBD // N_HEAD
        B, T = (2, 256)
        key = jax.random.key(seed)
        k1, k2, k3 = jax.random.split(key, 3)
        x = jax.random.normal(k1, (B, T, N_EMBD), dtype=jnp.float32)
        W_gate = jax.random.normal(k2, (N_HEAD, N_EMBD), dtype=jnp.float32) * 0.02
        W_qkv = jax.random.normal(k3, (3 * N_EMBD, N_EMBD), dtype=jnp.float32) * 0.02
        return {'x': x, 'W_gate': W_gate, 'W_qkv': W_qkv}
    _L0_ffn_all = _L0_ffn_setup()
    _L0_ffn_in = {k: v for k, v in _L0_ffn_all.items() if k in ('W_gate', 'W_qkv')}
    del _L0_ffn_all
    return {'x': x, 'ctx_1024': ctx_1024, 'L0_xattn_Wq': _L0_xattn_in['Wq'], 'L0_xattn_Wk': _L0_xattn_in['Wk'], 'L0_xattn_Wv': _L0_xattn_in['Wv'], 'L0_xattn_Wo': _L0_xattn_in['Wo'], 'L0_xattn_gq': _L0_xattn_in['gq'], 'L0_xattn_gk': _L0_xattn_in['gk'], 'L0_attn_W_qkv': _L0_attn_in['W_qkv'], 'L0_attn_W_out': _L0_attn_in['W_out'], 'L0_attn_b_out': _L0_attn_in['b_out'], 'L0_ffn_W_gate': _L0_ffn_in['W_gate'], 'L0_ffn_W_qkv': _L0_ffn_in['W_qkv']}

def reference(x, ctx_1024, L0_xattn_Wq, L0_xattn_Wk, L0_xattn_Wv, L0_xattn_Wo, L0_xattn_gq, L0_xattn_gk, L0_attn_W_qkv, L0_attn_W_out, L0_attn_b_out, L0_ffn_W_gate, L0_ffn_W_qkv):
    import jax
    import jax.numpy as jnp

    def _L0_xattn_ref(hidden_states, encoder_hidden_states, Wq, Wk, Wv, Wo, gq, gk):
        import jax, jax.numpy as jnp
        import numpy as np
        EPS = 1e-05

        def rmsnorm(x, g, eps=EPS):
            var = jnp.mean(jnp.square(x), axis=-1, keepdims=True)
            return x * jax.lax.rsqrt(var + eps) * g
        B, Sq, _ = hidden_states.shape
        Skv = encoder_hidden_states.shape[1]
        D = gq.shape[0]
        H = Wq.shape[1] // D
        scale = 1.0 / np.sqrt(D)
        q = (hidden_states @ Wq).reshape(B, Sq, H, D)
        k = (encoder_hidden_states @ Wk).reshape(B, Skv, H, D)
        v = (encoder_hidden_states @ Wv).reshape(B, Skv, H, D)
        q = rmsnorm(q, gq)
        k = rmsnorm(k, gk)
        scores = jnp.einsum('bqhd,bkhd->bhqk', q, k) * scale
        attn = jax.nn.softmax(scores, axis=-1)
        out = jnp.einsum('bhqk,bkhd->bqhd', attn, v)
        out = out.reshape(B, Sq, H * D)
        return out @ Wo

    def _L0_attn_ref(x, W_qkv, W_out, b_out):
        import jax, jax.numpy as jnp
        import numpy as np
        FP8_MAX = 448.0
        NUM_HEADS = 16

        def act_quant(x):
            scale = jnp.max(jnp.abs(x)) / FP8_MAX
            q = (x / scale).astype(jnp.float8_e4m3fn)
            return (q, scale)
        B, S, H = x.shape
        nH = NUM_HEADS
        hd = H // nH
        qkv = jnp.einsum('bsh,hf->bsf', x, W_qkv)
        qkv = qkv.reshape(B, S, 3, nH, hd)
        q = qkv[:, :, 0].transpose(0, 2, 1, 3)
        k = qkv[:, :, 1].transpose(0, 2, 1, 3)
        v = qkv[:, :, 2].transpose(0, 2, 1, 3)
        q8, q_scale = act_quant(q)
        k8, k_scale = act_quant(k)
        scores = jnp.einsum('bhqd,bhkd->bhqk', q8.astype(jnp.float32), k8.astype(jnp.float32))
        scores = scores * (q_scale * k_scale) / jnp.sqrt(jnp.float32(hd))
        attn = jax.nn.softmax(scores, axis=-1)
        v8, v_scale = act_quant(v)
        out = jnp.einsum('bhqk,bhkd->bhqd', attn, v8.astype(jnp.float32))
        out = out * v_scale
        out = out.transpose(0, 2, 1, 3).reshape(B, S, H)
        return jnp.einsum('bsh,ho->bso', out, W_out) + b_out

    def _L0_ffn_ref(x, W_gate, W_qkv):
        import jax, jax.numpy as jnp
        import numpy as np
        import math
        N_EMBD = 256
        N_HEAD = 16
        HEAD_DIM = N_EMBD // N_HEAD
        B, T = (2, 256)
        Bb, Tt, C = x.shape
        H, hd = (N_HEAD, HEAD_DIM)
        gating = jax.nn.softmax(x @ W_gate.T, axis=-1)
        idx = jnp.argmax(gating, axis=-1)
        indicator = jax.nn.one_hot(idx, H, dtype=gating.dtype)
        top1_val = jnp.max(gating, axis=-1, keepdims=True)
        gating_top1 = indicator * top1_val
        qkv = x @ W_qkv.T
        q, k, v = jnp.split(qkv, 3, axis=-1)
        k = k.reshape(Bb, Tt, H, hd)
        v = v.reshape(Bb, Tt, H, hd)
        k_shared = jnp.einsum('bth,bthd->btd', indicator, k)
        v_shared = jnp.einsum('bth,bthd->btd', gating_top1, v)
        q = q.reshape(Bb, Tt, H, hd).transpose(0, 2, 1, 3)
        att = jnp.einsum('bhqd,bkd->bhqk', q, k_shared) * (1.0 / math.sqrt(hd))
        causal = jnp.tril(jnp.ones((Tt, Tt), dtype=bool))
        att = jnp.where(causal[None, None, :, :], att, -jnp.inf)
        att = jax.nn.softmax(att, axis=-1)
        y = jnp.einsum('bhqk,bkd->bhqd', att, v_shared)
        y = y.transpose(0, 2, 1, 3).reshape(Bb, Tt, C)
        return y
    x = x + _L0_xattn_ref(_layernorm(x, axis=-1), ctx_1024, L0_xattn_Wq, L0_xattn_Wk, L0_xattn_Wv, L0_xattn_Wo, L0_xattn_gq, L0_xattn_gk)
    x = x + _L0_attn_ref(_layernorm(x, axis=-1), L0_attn_W_qkv, L0_attn_W_out, L0_attn_b_out)
    x = x + _L0_ffn_ref(_layernorm(x, axis=-1), L0_ffn_W_gate, L0_ffn_W_qkv)
    return x

_drawn_inputs = setup_inputs


def setup_inputs(seed=0):
    import zlib

    import numpy as np

    out = dict(_drawn_inputs(seed))
    spreads = {'L0_xattn_gq': (1.0, 0.2), 'L0_xattn_gk': (1.0, 0.2), 'L0_attn_b_out': (0.0, 0.1)}
    factors = {'L0_ffn_W_gate': 3.771, 'L0_ffn_W_qkv': 3.17}
    for name, (base, spread) in spreads.items():
        noise = np.random.default_rng([zlib.crc32(name.encode()), seed]).standard_normal(out[name].shape)
        drawn = base * np.exp(spread * noise) if base else spread * noise
        out[name] = jnp.asarray(drawn.astype(out[name].dtype))
    for name, factor in factors.items():
        out[name] = (out[name] * factor).astype(out[name].dtype)
    return out
```

```python
from collections import namedtuple
from contextlib import ExitStack

import concourse.bass as bass
import numpy as np
from concourse import mybir
from concourse.alu_op_type import AluOpType as ALU

F32 = mybir.dt.float32
F32R = mybir.dt.float32r
BF16 = mybir.dt.bfloat16
I32 = mybir.dt.int32
ACT = mybir.ActivationFunctionType
AX = mybir.AxisListType
ABSMAX = bass.bass_isa.ReduceOp.absmax

B, SQ, DIM = 16, 64, 256
SKV, CD = 1601, 128
H, D = 16, 128
INNER = H * D
HS, DS = 16, 16
P = 128
WC = DIM // P
NPAIR = B // 2
HQ = H * SQ
NT = -(-SKV // P)
ROWS = -(-SKV // NT)
FULL = SKV // NT
REST = SKV - FULL * NT
TP = 2 * NT
BANK = 512
HB = BANK // D
KC = INNER // BANK
EPS = 1e-5
SCALE = 1.0 / np.sqrt(D)
LIMIT = 60.0
FP8_MAX = 448.0
FAR = 1e30
CREDIT = 64
LN_EXP = "natural_log_exp_and_others"


def rows_of(n):
    return ROWS if n % NT < REST else FULL


def ring(length, slots, apart):
    whole = next(n for n in range(length // slots, -1, -1) if (length - n * slots) % apart == 0)
    return list(range(slots)) * whole + list(range(apart)) * ((length - whole * slots) // apart)


CT_SLOTS = 5
CT_SLOT = ring(TP, CT_SLOTS, 4)


PIECES = [slice(NT * n // 4, NT * (n + 1) // 4) for n in range(4)]


def ct_before(t):
    return next(k for k in range(1, TP) if CT_SLOT[(t - k) % TP] == CT_SLOT[t % TP])


def at(i, per, k):
    return per * i + (CREDIT + k)


class Shared:
    pass


def semaphores(nc, ctx, tag, names):
    return namedtuple(tag, names)(*(ctx.enter_context(nc.semaphore(f"{tag}_{n}")) for n in names.split()))


def alone(eng, sem):
    eng.sem_inc(sem, 1)


def over(ap, n):
    return ap.unsqueeze(len(ap.shape)).broadcast_to([*ap.shape, n])


def inverse_root_start(nc, dve, sem, x, total, n):
    nc.vector.tensor_scalar(x, total, 1.0 / n, EPS, ALU.mult, ALU.add).then_inc(sem, 1)


def inverse_root_guess(nc, act, S, i, log, y, x):
    act.wait_ge(S.x, at(i, 1, 1))
    nc.scalar.activation(log, x, ACT.Ln).then_inc(S.log, 1)
    act.wait_ge(S.log, at(i, 1, 1))
    nc.scalar.activation(y, log, ACT.Exp, scale=-0.5).then_inc(S.guess, 1)


def inverse_root_end(nc, dve, S, i, y, u, x, out):
    dve.wait_ge(S.guess, at(i, 1, 1))
    nc.vector.scalar_tensor_tensor(u, y, -0.5, y, ALU.mult, ALU.mult).then_inc(S.newton, 1)
    dve.wait_ge(S.newton, at(i, 2, 1))
    nc.vector.tensor_tensor(u, u, x, ALU.mult).then_inc(S.newton, 1)
    dve.wait_ge(S.newton, at(i, 2, 2))
    nc.vector.scalar_tensor_tensor(out, u, 1.5, y, ALU.add, ALU.mult).then_inc(S.root, 1)


ROOT = "x log guess newton root"



def primed(nc, ctx, plain, *loops):
    zero, made = semaphores(nc, ctx, *plain), [semaphores(nc, ctx, *group) for group in loops]
    with nc.Block() as block:
        @block.sync
        def _(sp):
            for group in (zero, *made):
                for sem in group:
                    sp.sem_clear(sem)
            for group in made:
                for sem in group:
                    sp.sem_inc(sem, CREDIT)
    return (zero, *made)


def setup(nc, T, psum, dram):
    with ExitStack() as ctx:
        g2 = ctx.enter_context(nc.sbuf_tensor("setup_g2", [P, 2], F32))
        gmax = ctx.enter_context(nc.sbuf_tensor("setup_gmax", [P, 2], F32))
        S, = primed(nc, ctx, ("setup", "x gains wk consts gprod gmax made split"))
        wk = T.big[:, 0:INNER]
        block = ctx.enter_context(nc.Block())

        @block.sync
        def _(sp):
            sp.dma_start(wk, dram["L0_xattn_Wk"]).then_inc(S.wk, 16)
            sp.dma_start(g2[:, 0:1], dram["L0_xattn_gq"].rearrange("(p a) -> p a", a=1)).then_inc(S.gains, 16)
            sp.dma_start(g2[:, 1:2], dram["L0_xattn_gk"].rearrange("(p a) -> p a", a=1)).then_inc(S.gains, 16)
            sp.dma_start(T.xs[:, :, :], dram["x"].rearrange("b q c -> (b q) c").rearrange("(n p) c -> p n c", p=P)).then_inc(S.x, 16)
            sp.wait_ge(S.x, 16)

        @block.gpsimd
        def _(pool):
            nc.gpsimd.memset(T.ident[:, :], 0.0).then_inc(S.consts, 1)
            pool.wait_ge(S.consts, 1)
            nc.gpsimd.affine_select(out=T.ident[:, :], in_=T.ident[:, :], compare_op=ALU.not_equal, fill=1.0,
                                    base=0, pattern=[[-1, P]], channel_multiplier=1).then_inc(S.consts, 1)
            nc.gpsimd.memset(T.ones[:, :], 1.0).then_inc(S.consts, 1)
            nc.gpsimd.memset(T.zero[:, :], 0.0).then_inc(S.consts, 1)
            pool.wait_ge(S.gprod, 1)
            nc.gpsimd.partition_all_reduce(gmax[:, 0:1], T.gcol[:, 0:1], P, ABSMAX).then_inc(S.gmax, 1)

        @block.vector
        def _(dve):
            dve.wait_ge(S.consts, 4)
            nc.vector.tensor_copy(T.identb[:, :], T.ident[:, :]).then_inc(S.made, 1)
            dve.wait_ge(S.wk, 16)
            nc.vector.tensor_copy(T.wkh[:, :], wk).then_inc(S.split, 1)
            dve.wait_ge(S.split, 1)
            nc.vector.tensor_tensor(T.wkl[:, :], wk, T.wkh[:, :].bitcast(F32), ALU.subtract).then_inc(S.split, 1)
            dve.wait_ge(S.gains, 32)
            nc.vector.tensor_tensor(T.gcol[:, 0:1], g2[:, 0:1], g2[:, 1:2], ALU.mult).then_inc(S.gprod, 1)
            dve.wait_ge(S.gprod, 1)
            nc.vector.tensor_scalar(T.gcol[:, 1:2], T.gcol[:, 0:1], float(SCALE), None, ALU.mult).then_inc(S.made, 1)
            dve.wait_ge(S.gmax, 1)
            nc.vector.tensor_scalar(gmax[:, 1:2], gmax[:, 0:1], -float(np.sqrt(D)), LIMIT, ALU.mult, ALU.add).then_inc(S.made, 1)
            dve.wait_ge(S.made, 3)
            nc.vector.tensor_scalar(T.shift[:, :], gmax[:, 1:2], 0.0, None, ALU.min).then_inc(S.made, 1)



QUERY_SEMS = "stats moments centred lnT lnTh lnTl qmm qcopy qsquare qsum qn qT qgh qgl qwmm qw"


def queries(nc, T, psum, dram):
    psT, psK, psS, psO, psM = psum
    with ExitStack() as ctx:
        def sb(name, shape, dt=F32):
            return ctx.enter_context(nc.sbuf_tensor(f"q_{name}", shape, dt))

        wqh, wql = sb("wqh", [P, WC, INNER], F32R), sb("wql", [P, WC, INNER], F32R)
        wkTh, wkTl = sb("wkTh", [P, H, CD], F32R), sb("wkTl", [P, H, CD], F32R)
        stats, mv = sb("stats", [P, 6]), sb("mv", [P, 2])
        lx = sb("lx", [P, 5, 1])
        xn = sb("xn", [P, WC, P])
        xTh, xTl = sb("xTh", [P, WC, P], F32R), sb("xTl", [P, WC, P], F32R)
        q = sb("q", [P, INNER])
        sq = sb("sq", [P, INNER])
        ss = sb("ss", [P, 6, H])
        qgh, qgl = sb("qgh", [P, INNER], F32R), sb("qgl", [P, INNER], F32R)
        W, S, L, R = primed(nc, ctx, ("wq", "wq0 wq1 wkT wkTh wkTl split passed"), ("query", QUERY_SEMS), ("queryln", ROOT), ("queryrms", ROOT))
        wk = T.big[:, 0:INNER]
        wq = T.big[:, INNER:(1 + WC) * INNER].rearrange("p (k n) -> p k n", k=WC)
        block = ctx.enter_context(nc.Block())

        @block.sync
        def _(sp):
            for k, sem in enumerate((W.wq0, W.wq1)):
                sp.dma_start(wq[:, k, :], dram["L0_xattn_Wq"][k * P:(k + 1) * P, :]).then_inc(sem, 16)

        @block.tensor
        def _(pe):
            for g in range(KC):
                if g >= 2:
                    pe.wait_ge(W.wkTl, g - 1)
                for h in range(HB):
                    last = nc.tensor.transpose(psK[:, g % 2, h * P:(h + 1) * P],
                                               wk[:, (HB * g + h) * P:(HB * g + h + 1) * P], T.ident[:, :])
                last.then_inc(W.wkT, 1)
            pe.wait_ge(W.wkTl, KC)
            pe.wait_ge(W.split, 4)
            with pe.Fori(0, NPAIR) as i:
                pe.wait_ge(S.centred, at(i, 1, 1))
                pe.wait_ge(S.lnTl, at(i, 1, 0))
                for k in range(WC):
                    last = nc.tensor.transpose(psT[:, k * P:(k + 1) * P], xn[:, k, :], T.ident[:, :])
                last.then_inc(S.lnT, 1)
                pe.wait_ge(S.lnTl, at(i, 1, 1))
                for c in range(KC):
                    pe.wait_ge(S.qsquare, at(i, KC, c - 1))
                    cols = slice(c * BANK, (c + 1) * BANK)
                    n = 0
                    for k in range(WC):
                        for x, w in ((xTh, wqh), (xTh, wql), (xTl, wqh)):
                            last = nc.tensor.matmul(psK[:, c % 2, :], x[:, k, :], w[:, k, cols],
                                                    start=(n == 0), stop=(n == 3 * WC - 1))
                            n += 1
                    last.then_inc(S.qmm, 1)
                for g in range(KC):
                    pe.wait_ge(S.qn, at(i, KC, g + 1))
                    pe.wait_ge(S.qgl, at(i, KC, g - 1))
                    for h in range(HB):
                        last = nc.tensor.transpose(psS[:, g % 2, h * P:(h + 1) * P],
                                                   q[:, (HB * g + h) * P:(HB * g + h + 1) * P], T.ident[:, :])
                    last.then_inc(S.qT, 1)
                for g in range(KC):
                    pe.wait_ge(S.qgl, at(i, KC, g + 1))
                    pe.wait_ge(S.qw, at(i, KC, g - 1))
                    for h in range(HB):
                        cols = slice((HB * g + h) * P, (HB * g + h + 1) * P)
                        for n, (w, x) in enumerate(((wkTh, qgh), (wkTh, qgl), (wkTl, qgh))):
                            last = nc.tensor.matmul(psO[:, g % 2, h * P:(h + 1) * P], w[:, HB * g + h, :], x[:, cols],
                                                    start=(n == 0), stop=(n == 2))
                    last.then_inc(S.qwmm, 1)

        @block.scalar
        def _(act):
            nc.scalar.preload_act_table_set(LN_EXP)
            for g in range(KC):
                act.wait_ge(W.wkT, g + 1)
                nc.scalar.activation(wkTh[:, HB * g:HB * (g + 1), :], psK[:, g % 2, :].rearrange("p (h c) -> p h c", c=CD),
                                     ACT.Copy).then_inc(W.wkTh, 1)
            with act.Fori(0, NPAIR) as i:
                inverse_root_guess(nc, act, L, i, lx[:, 1, :], lx[:, 2, :], lx[:, 0, :])
                act.wait_ge(S.lnT, at(i, 1, 1))
                nc.scalar.activation(xTh[:, :, :], psT[:, 0:WC * P].rearrange("p (k n) -> p k n", k=WC), ACT.Copy).then_inc(S.lnTh, 1)
                for c in range(KC):
                    cols = slice(c * BANK, (c + 1) * BANK)
                    act.wait_ge(S.qmm, at(i, KC, c + 1))
                    act.wait_ge(S.qT, at(i, KC, c + 1 - KC))
                    nc.scalar.activation(q[:, cols], psK[:, c % 2, :], ACT.Copy).then_inc(S.qcopy, 1)
                    act.wait_ge(S.qsum, at(i, 2, c // 2 - 1))
                    nc.scalar.activation(sq[:, cols], psK[:, c % 2, :], ACT.Square).then_inc(S.qsquare, 1)
                inverse_root_guess(nc, act, R, i, ss[:, 2, :], ss[:, 3, :], ss[:, 1, :])
                for g in range(KC):
                    cols = slice(g * BANK, (g + 1) * BANK)
                    act.wait_ge(S.qT, at(i, KC, g + 1))
                    act.wait_ge(S.qwmm, at(i, KC, g + 1 - KC))
                    nc.scalar.activation(qgh[:, cols], psS[:, g % 2, :], ACT.Copy, scale=T.gcol[:, 1:2]).then_inc(S.qgh, 1)
                for g in range(KC):
                    act.wait_ge(S.qwmm, at(i, KC, g + 1))
                    for b in range(2):
                        dst = T.queries[:, bass.ds(i, 1), b, HB * g:HB * (g + 1), :].rearrange("p n h q -> p (n h) q")
                        src = psO[:, g % 2, :].rearrange("p (h b q) -> p h b q", b=2, q=SQ)[:, :, b, :]
                        last = nc.scalar.activation(dst, src, ACT.Copy)
                    last.then_inc(S.qw, 1)

        @block.vector
        def _(dve):
            for g in range(KC):
                dve.wait_ge(W.wkTh, g + 1)
                nc.vector.tensor_tensor(wkTl[:, HB * g:HB * (g + 1), :], psK[:, g % 2, :].rearrange("p (h c) -> p h c", c=CD),
                                        wkTh[:, HB * g:HB * (g + 1), :].bitcast(F32), ALU.subtract).then_inc(W.wkTl, 1)
            for k, sem in enumerate((W.wq0, W.wq1)):
                dve.wait_ge(sem, 16)
                nc.vector.tensor_copy(wqh[:, k, :], wq[:, k, :]).then_inc(W.split, 1)
                dve.wait_ge(W.split, 2 * k + 1)
                nc.vector.tensor_tensor(wql[:, k, :], wq[:, k, :], wqh[:, k, :].bitcast(F32), ALU.subtract).then_inc(W.split, 1)
            with dve.Fori(0, NPAIR) as i:
                x = T.xs[:, bass.ds(i, 1), :].rearrange("p n c -> p (n c)")
                nc.vector.bn_stats(stats[:, :], x).then_inc(S.stats, 1)
                dve.wait_ge(S.stats, at(i, 1, 1))
                alone(dve, W.passed)
                nc.vector.bn_aggr(mv[:, :], stats[:, :]).then_inc(S.moments, 1)
                dve.wait_ge(S.moments, at(i, 1, 1))
                inverse_root_start(nc, dve, L.x, lx[:, 0, :], mv[:, 1:2], 1)
                inverse_root_end(nc, dve, L, i, lx[:, 2, :], lx[:, 3, :], lx[:, 0, :], lx[:, 4, :])
                dve.wait_ge(L.root, at(i, 1, 1))
                dve.wait_ge(S.lnT, at(i, 1, 0))
                nc.vector.tensor_scalar(xn[:, :, :].rearrange("p k n -> p (k n)"), x, mv[:, 0:1], lx[:, 4, :],
                                        ALU.subtract, ALU.mult).then_inc(S.centred, 1)
                dve.wait_ge(S.lnTh, at(i, 1, 1))
                dve.wait_ge(S.qmm, at(i, KC, 0))
                nc.vector.tensor_tensor(xTl[:, :, :], psT[:, 0:WC * P].rearrange("p (k n) -> p k n", k=WC),
                                        xTh[:, :, :].bitcast(F32), ALU.subtract).then_inc(S.lnTl, 1)
                for k in range(2):
                    dve.wait_ge(S.qsquare, at(i, KC, 2 * k + 2))
                    nc.vector.tensor_reduce(ss[:, 0, 8 * k:8 * k + 8], sq[:, k * 2 * BANK:(k + 1) * 2 * BANK]
                                            .rearrange("p (h d) -> p h d", d=D), AX.X, ALU.add).then_inc(S.qsum, 1)
                dve.wait_ge(S.qsum, at(i, 2, 2))
                inverse_root_start(nc, dve, R.x, ss[:, 1, :], ss[:, 0, :], D)
                inverse_root_end(nc, dve, R, i, ss[:, 3, :], ss[:, 4, :], ss[:, 1, :], ss[:, 5, :])
                dve.wait_ge(R.root, at(i, 1, 1))
                for g in range(KC):
                    cols = q[:, g * BANK:(g + 1) * BANK].rearrange("p (h d) -> p h d", d=D)
                    nc.vector.tensor_tensor(cols, cols, over(ss[:, 5, HB * g:HB * (g + 1)], D), ALU.mult).then_inc(S.qn, 1)
                for g in range(KC):
                    cols = slice(g * BANK, (g + 1) * BANK)
                    dve.wait_ge(S.qgh, at(i, KC, g + 1))
                    nc.vector.scalar_tensor_tensor(qgl[:, cols], psS[:, g % 2, :], T.gcol[:, 1:2], qgh[:, cols].bitcast(F32),
                                                   ALU.mult, ALU.subtract).then_inc(S.qgl, 1)



MAIN_SEMS = "ct cth ctl kmm ksq ksum smm zz expd phi pl acc vmm nath nat qh ql oev_a oev_d den rden"


def cross_attention(nc, T, psum, dram):
    psT, psK, psS, psO, psM = psum
    with ExitStack() as ctx:
        def sb(name, shape, dt=F32):
            return ctx.enter_context(nc.sbuf_tensor(f"c_{name}", shape, dt))

        raw = sb("raw", [ROWS, 2, NT, CD])
        ch, cl = sb("ch", [ROWS, 2, NT, CD], F32R), sb("cl", [ROWS, 2, NT, CD], F32R)
        cTh, cTl = sb("cTh", [CD, CT_SLOTS, ROWS], F32R), sb("cTl", [CD, CT_SLOTS, ROWS], F32R)
        qwh, qwl = sb("qwh", [CD, 2, HQ], F32R), sb("qwl", [CD, 2, HQ], F32R)
        sq = sb("sq", [ROWS, 2, INNER])
        ss = sb("ss", [ROWS, 2, 6, H])
        prob = sb("prob", [ROWS, 2, HQ])
        ph, pl = sb("ph", [ROWS, 2, HQ], F32R), sb("pl", [ROWS, 2, HQ], F32R)
        acc = sb("acc", [ROWS, 2, HQ])
        W, S, R = primed(nc, ctx, ("wc", "zeroed loaded00 loaded01 loaded10 loaded11 passed"), ("main", MAIN_SEMS), ("keyrms", ROOT))
        loaded = ((W.loaded00, W.loaded01), (W.loaded10, W.loaded11))
        block = ctx.enter_context(nc.Block())
        ctx_rows = dram["ctx_1024"]

        def done(i, t, per, k=None):
            return at(i, per * TP, per * t + (per if k is None else k))

        def batch_done(i, batch, per=1, k=None):
            return at(i, 2 * per, per * batch + (per if k is None else k))

        def more(i, batch):
            return batch < 2 or not isinstance(i, int) or i < NPAIR - 1

        def steps(i, last):
            for t in range(TP):
                yield tuple(u if not last or u < TP else None for u in (t, t + 2, t + 3, t + 4, t + 5))

        def pipeline(eng, emit):
            for t in range(-5, 0):
                emit(0, *(u if u >= 0 else None for u in (t, t + 2, t + 3, t + 4, t + 5)))
            with eng.Fori(0, NPAIR - 1) as i:
                for v in steps(i, False):
                    emit(i, *v)
            for v in steps(NPAIR - 1, True):
                emit(NPAIR - 1, *v)

        def out_half(i, batch, half):
            pair, b = i + batch // 2, batch % 2
            big = T.big[:, :].rearrange("p (n b m) -> p n b m", b=2, m=HQ)
            n = slice(pair, pair + 1) if isinstance(pair, int) else bass.ds(pair, 1)
            return big[:, n, b, half * BANK:(half + 1) * BANK].rearrange("p n m -> p (n m)")

        @block.sync
        def _(sp):
            sp.wait_ge(W.zeroed, 1)

            def load(i, b):
                one = ctx_rows[bass.ds(2 * i + b, 1)] if not isinstance(i, int) else ctx_rows[2 * i + b:2 * i + b + 1]
                sp.dma_start(raw[0:FULL, b, :, :], one[:, 0:FULL * NT, :].rearrange("n (p t) c -> p (n t) c", t=NT))\
                  .then_inc(loaded[b][0], 16)
                sp.dma_start(raw[FULL:ROWS, b, 0:REST, :], one[:, FULL * NT:SKV, :]).then_inc(loaded[b][1], 16)

            for b in range(2):
                load(0, b)
            with sp.Fori(0, NPAIR - 1) as i:
                for b in range(2):
                    sp.wait_ge(S.ct, done(i, NT * (b + 1) - 1, 1))
                    alone(sp, W.passed)
                    sp.wait_ge(S.nat, batch_done(i, b, len(PIECES)))
                    load(i + 1, b)

        @block.tensor
        def _(pe):
            def key_chunk(i, k, c):
                slot = CT_SLOT[k % TP]
                if c == 0:
                    pe.wait_ge(S.ctl, done(i, k, 1))
                pe.wait_ge(S.ksq, done(i, k, KC, c - 1))
                cols = slice(c * BANK, (c + 1) * BANK)
                for n, (x, w) in enumerate(((cTh, T.wkh), (cTh, T.wkl), (cTl, T.wkh))):
                    last = nc.tensor.matmul(psK[0:ROWS, c % 2, :], x[:, slot, :], w[:, cols], start=(n == 0), stop=(n == 2))
                last.then_inc(S.kmm, 1)

            def score_half(i, s, half):
                slot, b = CT_SLOT[s % TP], s % TP // NT
                if s % NT == 0 and half == 0:
                    pe.wait_ge(S.qh, batch_done(i, s // NT))
                    pe.wait_ge(S.ql, batch_done(i, s // NT))
                pe.wait_ge(S.zz, done(i, s, 2, half - 1))
                cols = slice(half * BANK, (half + 1) * BANK)
                for n, (x, w) in enumerate(((cTh, qwh), (cTh, qwl), (cTl, qwh))):
                    last = nc.tensor.matmul(psS[0:ROWS, half, :], x[:, slot, :], w[:, b, cols], start=(n == 0), stop=(n == 2))
                last.then_inc(S.smm, 1)

            def weigh_half(i, v, half):
                b, tile, rows = v // NT, v % NT, rows_of(v)
                if half == 0:
                    pe.wait_ge(S.pl, done(i, v, 1))
                    if tile == 0:
                        pe.wait_ge(S.nat, batch_done(i, b, len(PIECES)))
                        pe.wait_ge(S.oev_a, batch_done(i, b - 1))
                        pe.wait_ge(S.oev_d, batch_done(i, b - 1))
                cols = slice(half * BANK, (half + 1) * BANK)
                for n, (x, w) in enumerate(((ch, ph), (ch, pl), (cl, ph))):
                    last = nc.tensor.matmul(psO[:, half, :], x[0:rows, b, tile, :], w[0:rows, v % 2, cols],
                                            start=(tile == 0 and n == 0), stop=(tile == NT - 1 and n == 2))
                if half:
                    last.then_inc(S.vmm, 1)

            def denominators(i, b):
                pe.wait_ge(S.acc, done(i, NT * (b + 1) - 1, 1))
                if b == 0:
                    pe.wait_ge(S.rden, at(i, 1, 0))
                for h in range(H):
                    last = nc.tensor.matmul(psM[b * SQ:(b + 1) * SQ, h:h + 1], acc[:, b, h * SQ:(h + 1) * SQ],
                                            T.ones[0:ROWS, 0:1], start=True, stop=True)
                last.then_inc(S.den, 1)

            def step(i, v, s, r, k, x):
                if x is not None:
                    if x % NT == 0:
                        pair, b = x // TP, x % TP // NT
                        for k2 in range(2):
                            pe.wait_ge(loaded[b][k2], 16 * i + 16 * (pair + 1))
                    pe.wait_ge(S.ctl, done(i, x - 1, 1))
                    nc.tensor.transpose(psT[:, 0:ROWS], raw[:, x % TP // NT, x % NT, :],
                                        T.ident[0:ROWS, 0:ROWS]).then_inc(S.ct, 1)
                if k is not None:
                    key_chunk(i, k, 0)
                if s is not None:
                    score_half(i, s, 0)
                if k is not None:
                    key_chunk(i, k, 1)
                if s is not None:
                    score_half(i, s, 1)
                if k is not None:
                    key_chunk(i, k, 2)
                if v is not None:
                    weigh_half(i, v, 0)
                if k is not None:
                    key_chunk(i, k, 3)
                if v is not None:
                    weigh_half(i, v, 1)
                if v is not None and v % NT == NT - 1:
                    denominators(i, v // NT)

            pipeline(pe, step)

        @block.scalar
        def _(act):
            nc.scalar.preload_act_table_set(LN_EXP)

            def square(i, k, c):
                act.wait_ge(S.kmm, done(i, k, KC, c + 1))
                act.wait_ge(S.ksum, done(i, k - 2, 2, c // 2 + 1))
                nc.scalar.activation(sq[:, k % 2, c * BANK:(c + 1) * BANK], psK[0:ROWS, c % 2, :], ACT.Square).then_inc(S.ksq, 1)

            def exponentials(i, s):
                act.wait_ge(S.zz, done(i, s, 2))
                nc.scalar.activation(prob[:, s % 2, :], prob[:, s % 2, :], ACT.Exp, bias=T.shift[0:ROWS, :]).then_inc(S.expd, 1)

            def probs_high(i, s):
                act.wait_ge(S.expd, done(i, s, 1))
                act.wait_ge(S.vmm, done(i, s - 2, 1))
                nc.scalar.activation(ph[:, s % 2, :], prob[:, s % 2, :], ACT.Copy).then_inc(S.phi, 1)

            def query_high(i, batch):
                b = batch % 2
                act.wait_ge(S.smm, done(i, NT * (batch - 1) - 1, 2))
                pair = i + batch // 2
                src = T.queries[:, bass.ds(pair, 1), b, :, :] if not isinstance(pair, int) else T.queries[:, pair:pair + 1, b, :, :]
                nc.scalar.activation(qwh[:, b, :], src.rearrange("p n h q -> p (n h q)"), ACT.Copy).then_inc(S.qh, 1)

            def context_high(i, batch, piece):
                b = batch % 2
                if piece == 0:
                    for k2 in range(2):
                        act.wait_ge(loaded[b][k2], 16 * i + 16 * (batch // 2 + 1))
                    act.wait_ge(S.vmm, done(i, NT * (batch - 1) - 1, 1))
                nc.scalar.activation(ch[:, b, PIECES[piece], :], raw[:, b, PIECES[piece], :], ACT.Copy).then_inc(S.nath, 1)

            def step(i, v, s, r, k, x):
                e = s - 1 if s is not None and s > 0 else TP - 1 if s is None and v == TP - 2 else None
                if e is not None:
                    exponentials(i, e)
                if k is not None:
                    square(i, k, 0)
                if e is not None:
                    probs_high(i, e)
                if k is not None:
                    square(i, k, 1)
                if x is not None:
                    act.wait_ge(S.ct, done(i, x, 1))
                    act.wait_ge(S.smm, done(i, x - ct_before(x), 2))
                    nc.scalar.activation(cTh[:, CT_SLOT[x % TP], :], psT[:, 0:ROWS], ACT.Copy).then_inc(S.cth, 1)
                if r is not None:
                    n = at(i, TP, r) - CREDIT
                    inverse_root_guess(nc, act, R, n, ss[:, r % 2, 2, :], ss[:, r % 2, 3, :], ss[:, r % 2, 1, :])
                if k is not None:
                    square(i, k, 2)
                    square(i, k, 3)
                    if k % NT == NT - 2 and more(i, k // NT + 1):
                        query_high(i, k // NT + 1)
                    if k % NT - (NT - 6) in range(len(PIECES)) and more(i, k // NT + 1):
                        context_high(i, k // NT + 1, k % NT - (NT - 6))
                if v is not None and v % NT == NT - 1:
                    evacuate(i, v // NT)

            def evacuate(i, batch):
                act.wait_ge(S.vmm, done(i, NT * (batch + 1) - 1, 1))
                act.wait_ge(S.ql, batch_done(i, batch))
                alone(act, W.passed)
                dst = out_half(i, batch, 0)
                nc.scalar.activation(dst, psO[:, 0, :], ACT.Copy).then_inc(S.oev_a, 1)

            query_high(0, 0)
            for piece in range(len(PIECES)):
                context_high(0, 0, piece)
            pipeline(act, step)

        @block.vector
        def _(dve):
            nc.vector.memset(raw[:, :, :, :], 0.0).then_inc(W.zeroed, 1)

            def context_low(i, batch, piece):
                b = batch % 2
                dve.wait_ge(S.nath, batch_done(i, batch, len(PIECES), piece + 1))
                nc.vector.tensor_tensor(cl[:, b, PIECES[piece], :], raw[:, b, PIECES[piece], :],
                                        ch[:, b, PIECES[piece], :].bitcast(F32), ALU.subtract).then_inc(S.nat, 1)

            def query_low(i, batch):
                b = batch % 2
                dve.wait_ge(S.qh, batch_done(i, batch))
                dve.wait_ge(S.smm, done(i, NT * (batch - 1) - 1, 2))
                pair = i + batch // 2
                src = T.queries[:, bass.ds(pair, 1), b, :, :] if not isinstance(pair, int) else T.queries[:, pair:pair + 1, b, :, :]
                nc.vector.tensor_tensor(qwl[:, b, :], src.rearrange("p n h q -> p (n h q)"), qwh[:, b, :].bitcast(F32),
                                        ALU.subtract).then_inc(S.ql, 1)

            def key_sums(i, k, part):
                dve.wait_ge(S.ksq, done(i, k, KC, 2 * part + 2))
                dve.wait_ge(R.x, done(i, k - 2, 1))
                nc.vector.tensor_reduce(ss[:, k % 2, 0, 8 * part:8 * part + 8],
                                        sq[:, k % 2, part * 2 * BANK:(part + 1) * 2 * BANK].rearrange("p (h d) -> p h d", d=D),
                                        AX.X, ALU.add).then_inc(S.ksum, 1)

            def scale_scores(i, s, half):
                cols = slice(half * BANK, (half + 1) * BANK)
                if half == 0:
                    dve.wait_ge(R.root, done(i, s, 1))
                    dve.wait_ge(S.acc, done(i, s - 2, 1))
                dve.wait_ge(S.smm, done(i, s, 2, half + 1))
                nc.vector.tensor_tensor(prob[:, s % 2, cols].rearrange("p (h q) -> p h q", q=SQ),
                                        psS[0:ROWS, half, :].rearrange("p (h q) -> p h q", q=SQ),
                                        over(ss[:, s % 2, 5, 8 * half:8 * half + 8], SQ), ALU.mult).then_inc(S.zz, 1)

            def evacuate(i, batch):
                dve.wait_ge(S.vmm, done(i, NT * (batch + 1) - 1, 1))
                nc.vector.tensor_copy(out_half(i, batch, 1), psO[:, 1, :]).then_inc(S.oev_d, 1)

            def step(i, v, s, r, k, x):
                if r is not None:
                    key_sums(i, r, 1)
                    dve.wait_ge(S.ksum, done(i, r, 2))
                    inverse_root_start(nc, dve, R.x, ss[:, r % 2, 1, :], ss[:, r % 2, 0, :], D)
                if s is not None:
                    scale_scores(i, s, 0)
                if k is not None:
                    key_sums(i, k, 0)
                if x is not None:
                    dve.wait_ge(S.cth, done(i, x, 1))
                    dve.wait_ge(S.smm, done(i, x - ct_before(x), 2))
                    nc.vector.tensor_tensor(cTl[:, CT_SLOT[x % TP], :], psT[:, 0:ROWS], cTh[:, CT_SLOT[x % TP], :].bitcast(F32),
                                            ALU.subtract).then_inc(S.ctl, 1)
                if s is not None:
                    scale_scores(i, s, 1)
                if r is not None:
                    n = at(i, TP, r) - CREDIT
                    inverse_root_end(nc, dve, R, n, ss[:, r % 2, 3, :], ss[:, r % 2, 4, :], ss[:, r % 2, 1, :], ss[:, r % 2, 5, :])
                if k is not None:
                    if k % NT == NT - 1 and more(i, k // NT + 1):
                        query_low(i, k // NT + 1)
                    if k % NT - (NT - 5) in range(len(PIECES)) and more(i, k // NT + 1):
                        context_low(i, k // NT + 1, k % NT - (NT - 5))
                if v is not None and v % NT == NT - 1:
                    evacuate(i, v // NT)
                if v is not None and v == TP - 1:
                    dve.wait_ge(S.den, batch_done(i, 1))
                    n = slice(i, i + 1) if isinstance(i, int) else bass.ds(i, 1)
                    nc.vector.reciprocal(T.rden[:, n, :].rearrange("p n h -> p (n h)"), psM[:, 0:H]).then_inc(S.rden, 1)

            for piece in range(len(PIECES)):
                context_low(0, 0, piece)
            query_low(0, 0)
            pipeline(dve, step)

        @block.gpsimd
        def _(pool):
            def step(i, v, s, r, k, x):
                if s is not None and s > 0:
                    low_and_sum(i, s - 1)
                elif s is None and v == TP - 2:
                    low_and_sum(i, TP - 1)

            def low_and_sum(i, s):
                batch, rows = s // NT, rows_of(s)
                pool.wait_ge(S.phi, done(i, s, 1))
                pool.wait_ge(S.vmm, done(i, s - 2, 1))
                nc.gpsimd.tensor_tensor(pl[:, s % 2, :], prob[:, s % 2, :], ph[:, s % 2, :].bitcast(F32), ALU.subtract).then_inc(S.pl, 1)
                if s % NT == 0:
                    pool.wait_ge(S.den, at(i, 2, batch - 1))
                    nc.gpsimd.tensor_tensor(acc[:, batch % 2, :], prob[:, s % 2, :], T.zero[0:ROWS, :].broadcast_to([ROWS, HQ]), ALU.add).then_inc(S.acc, 1)
                else:
                    pool.wait_ge(S.acc, done(i, s - 1, 1))
                    nc.gpsimd.tensor_tensor(acc[0:rows, batch % 2, :], acc[0:rows, batch % 2, :], prob[0:rows, s % 2, :], ALU.add).then_inc(S.acc, 1)

            pipeline(pool, step)



OUT_SEMS = ("oh ol vmm av avT avh avl wo x2 stats moments centred lnT lnTh lnTl qkvmm qkv_a qkv_b amax")


def project(nc, T, psum, dram):
    psT, psK, psS, psO, psM = psum
    with ExitStack() as ctx:
        def sb(name, shape, dt=F32):
            return ctx.enter_context(nc.sbuf_tensor(f"o_{name}", shape, dt))

        wvh, wvl = sb("wvh", [P, INNER], F32R), sb("wvl", [P, INNER], F32R)
        woh, wol = sb("woh", [P, H, DIM], F32R), sb("wol", [P, H, DIM], F32R)
        wqkv = sb("wqkv", [P, WC, 3 * DIM])
        wqkvh, wqkvl = sb("wqkvh", [P, WC, 3 * DIM], F32R), sb("wqkvl", [P, WC, 3 * DIM], F32R)
        oh, ol = sb("oh", [P, H, 2, SQ], F32R), sb("ol", [P, H, 2, SQ], F32R)
        av = sb("av", [P, INNER])
        avh, avl = sb("avh", [P, INNER], F32R), sb("avl", [P, INNER], F32R)
        stats, mv, lx = sb("stats", [P, 6]), sb("mv", [P, 2]), sb("lx", [P, 5, 1])
        xn = sb("xn", [P, WC, P])
        xTh, xTl = sb("xTh", [P, WC, P], F32R), sb("xTl", [P, WC, P], F32R)
        W, S, L = primed(nc, ctx, ("wo", "wv wo wqkv high low passed"), ("out", OUT_SEMS), ("outln", ROOT))
        flat = T.qkv[:, :, :].rearrange("p n m -> p (n m)")
        wv = flat[:, 0:INNER]
        wo = flat[:, INNER:INNER + H * DIM]
        block = ctx.enter_context(nc.Block())

        @block.sync
        def _(sp):
            sp.dma_start(wv, dram["L0_xattn_Wv"]).then_inc(W.wv, 16)
            sp.dma_start(wo.rearrange("p (h n) -> p h n", h=H), dram["L0_xattn_Wo"].rearrange("(h p) n -> p h n", p=P)).then_inc(W.wo, 16)
            sp.dma_start(wqkv[:, :, :], dram["L0_attn_W_qkv"].rearrange("(k p) n -> p k n", p=P)).then_inc(W.wqkv, 16)

        halves = ((wv, wvh[:, :], wvl[:, :], W.wv),
                  (wo, woh[:, :, :].rearrange("p h n -> p (h n)"), wol[:, :, :].rearrange("p h n -> p (h n)"), W.wo),
                  (wqkv[:, :, :].rearrange("p k n -> p (k n)"), wqkvh[:, :, :].rearrange("p k n -> p (k n)"),
                   wqkvl[:, :, :].rearrange("p k n -> p (k n)"), W.wqkv))

        @block.tensor
        def _(pe):
            pe.wait_ge(W.low, len(halves))
            with pe.Fori(0, NPAIR) as i:
                pe.wait_ge(S.ol, at(i, 1, 1))
                for g in range(KC):
                    pe.wait_ge(S.av, at(i, KC, g - 1))
                    for h in range(HB):
                        cols = slice((HB * g + h) * P, (HB * g + h + 1) * P)
                        for n, (x, w) in enumerate(((oh, wvh), (oh, wvl), (ol, wvh))):
                            last = nc.tensor.matmul(psK[:, g % 2, h * P:(h + 1) * P],
                                                    x[:, HB * g + h, :, :].rearrange("p b q -> p (b q)"), w[:, cols],
                                                    start=(n == 0), stop=(n == 2))
                    last.then_inc(S.vmm, 1)
                for g in range(KC):
                    pe.wait_ge(S.av, at(i, KC, g + 1))
                    pe.wait_ge(S.avl, at(i, KC, g - 1))
                    for h in range(HB):
                        last = nc.tensor.transpose(psS[:, g % 2, h * P:(h + 1) * P],
                                                   av[:, (HB * g + h) * P:(HB * g + h + 1) * P], T.ident[:, :])
                    last.then_inc(S.avT, 1)
                pe.wait_ge(S.x2, at(i, 1, 0))
                for h in range(H):
                    if h % HB == 0:
                        pe.wait_ge(S.avl, at(i, KC, h // HB + 1))
                    cols = slice(h * P, (h + 1) * P)
                    for n, (x, w) in enumerate(((avh, woh), (avh, wol), (avl, woh))):
                        last = nc.tensor.matmul(psO[:, 0, 0:DIM], x[:, cols], w[:, h, :],
                                                start=(h == 0 and n == 0), stop=(h == H - 1 and n == 2))
                last.then_inc(S.wo, 1)
                pe.wait_ge(S.centred, at(i, 1, 1))
                for k in range(WC):
                    last = nc.tensor.transpose(psT[:, k * P:(k + 1) * P], xn[:, k, :], T.ident[:, :])
                last.then_inc(S.lnT, 1)
                pe.wait_ge(S.lnTl, at(i, 1, 1))
                pe.wait_ge(S.amax, at(i, 2, 0))
                for cols, out in ((slice(0, 2 * DIM), psO[:, 1, :]), (slice(2 * DIM, 3 * DIM), psM[:, 0:DIM])):
                    n = 0
                    for k in range(WC):
                        for x, w in ((xTh, wqkvh), (xTh, wqkvl), (xTl, wqkvh)):
                            last = nc.tensor.matmul(out, x[:, k, :], w[:, k, cols], start=(n == 0), stop=(n == 3 * WC - 1))
                            n += 1
                    last.then_inc(S.qkvmm, 1)

        @block.scalar
        def _(act):
            nc.scalar.preload_act_table_set(LN_EXP)
            for n, (full, high, low, sem) in enumerate(halves):
                act.wait_ge(sem, 16)
                nc.scalar.activation(high, full, ACT.Copy).then_inc(W.high, 1)
            act.wait_ge(W.low, len(halves))
            with act.Fori(0, NPAIR) as i:
                act.wait_ge(S.vmm, at(i, KC, 0))
                for b in range(2):
                    src = T.queries[:, bass.ds(i, 1), b, :, :].rearrange("p n h q -> p (n h) q")
                    last = nc.scalar.activation(oh[:, :, b, :], src, ACT.Copy)
                last.then_inc(S.oh, 1)
                for g in range(KC):
                    cols = slice(g * BANK, (g + 1) * BANK)
                    act.wait_ge(S.avT, at(i, KC, g + 1))
                    act.wait_ge(S.wo, at(i, 1, 0))
                    nc.scalar.activation(avh[:, cols], psS[:, g % 2, :], ACT.Copy).then_inc(S.avh, 1)
                inverse_root_guess(nc, act, L, i, lx[:, 1, :], lx[:, 2, :], lx[:, 0, :])
                act.wait_ge(S.lnT, at(i, 1, 1))
                act.wait_ge(S.qkvmm, at(i, 2, 0))
                nc.scalar.activation(xTh[:, :, :], psT[:, 0:WC * P].rearrange("p (k n) -> p k n", k=WC), ACT.Copy).then_inc(S.lnTh, 1)
                act.wait_ge(S.qkvmm, at(i, 2, 1))
                nc.scalar.activation(T.qkv[:, bass.ds(i, 1), 0:2 * DIM].rearrange("p n m -> p (n m)"), psO[:, 1, :], ACT.Copy).then_inc(S.qkv_a, 1)
                act.wait_ge(S.qkvmm, at(i, 2, 2))
                nc.scalar.activation(T.qkv[:, bass.ds(i, 1), 2 * DIM:3 * DIM].rearrange("p n m -> p (n m)"), psM[:, 0:DIM], ACT.Copy).then_inc(S.qkv_b, 1)

        @block.vector
        def _(dve):
            for n, (full, high, low, sem) in enumerate(halves):
                dve.wait_ge(W.high, n + 1)
                nc.vector.tensor_tensor(low, full, high.bitcast(F32), ALU.subtract).then_inc(W.low, 1)
            with dve.Fori(0, NPAIR) as i:
                dve.wait_ge(S.oh, at(i, 1, 1))
                for b in range(2):
                    src = T.queries[:, bass.ds(i, 1), b, :, :].rearrange("p n h q -> p (n h) q")
                    last = nc.vector.tensor_tensor(ol[:, :, b, :], src, oh[:, :, b, :].bitcast(F32), ALU.subtract)
                last.then_inc(S.ol, 1)
                for g in range(KC):
                    dve.wait_ge(S.vmm, at(i, KC, g + 1))
                    dve.wait_ge(S.avT, at(i, KC, g + 1 - KC))
                    cols = slice(g * BANK, (g + 1) * BANK)
                    rden = T.rden[:, bass.ds(i, 1), HB * g:HB * (g + 1)].rearrange("p n h -> p (n h)")
                    nc.vector.tensor_tensor(av[:, cols].rearrange("p (h d) -> p h d", d=D),
                                            psK[:, g % 2, :].rearrange("p (h d) -> p h d", d=D), over(rden, D), ALU.mult).then_inc(S.av, 1)
                for g in range(KC):
                    cols = slice(g * BANK, (g + 1) * BANK)
                    dve.wait_ge(S.avh, at(i, KC, g + 1))
                    nc.vector.tensor_tensor(avl[:, cols], psS[:, g % 2, :], avh[:, cols].bitcast(F32), ALU.subtract).then_inc(S.avl, 1)
                x = T.xs[:, bass.ds(i, 1), :].rearrange("p n c -> p (n c)")
                dve.wait_ge(S.wo, at(i, 1, 1))
                nc.vector.tensor_tensor(x, x, psO[:, 0, 0:DIM], ALU.add).then_inc(S.x2, 1)
                dve.wait_ge(S.x2, at(i, 1, 1))
                alone(dve, W.passed)
                nc.vector.bn_stats(stats[:, :], x).then_inc(S.stats, 1)
                dve.wait_ge(S.stats, at(i, 1, 1))
                alone(dve, W.passed)
                nc.vector.bn_aggr(mv[:, :], stats[:, :]).then_inc(S.moments, 1)
                dve.wait_ge(S.moments, at(i, 1, 1))
                inverse_root_start(nc, dve, L.x, lx[:, 0, :], mv[:, 1:2], 1)
                inverse_root_end(nc, dve, L, i, lx[:, 2, :], lx[:, 3, :], lx[:, 0, :], lx[:, 4, :])
                dve.wait_ge(L.root, at(i, 1, 1))
                nc.vector.tensor_scalar(xn[:, :, :].rearrange("p k n -> p (k n)"), x, mv[:, 0:1], lx[:, 4, :],
                                        ALU.subtract, ALU.mult).then_inc(S.centred, 1)
                dve.wait_ge(S.lnTh, at(i, 1, 1))
                nc.vector.tensor_tensor(xTl[:, :, :], psT[:, 0:WC * P].rearrange("p (k n) -> p k n", k=WC),
                                        xTh[:, :, :].bitcast(F32), ALU.subtract).then_inc(S.lnTl, 1)
                amax = T.amax[:, bass.ds(i, 1), :].rearrange("p n g -> p (n g)")
                dve.wait_ge(S.qkv_a, at(i, 1, 1))
                nc.vector.tensor_reduce(amax[:, 0:2], psO[:, 1, :].rearrange("p (g n) -> p g n", g=2), AX.X, ALU.max,
                                        apply_absolute_value=True).then_inc(S.amax, 1)
                dve.wait_ge(S.qkv_b, at(i, 1, 1))
                nc.vector.tensor_reduce(amax[:, 2:3], psM[:, 0:DIM], AX.X, ALU.max, apply_absolute_value=True).then_inc(S.amax, 1)



HH = P // DS
NC = HS // HH
SM_SEMS = "smm smax sub exp total inv pT pTe vbd pv"
ATT_SEMS = "u expo magic sum q8 T qT kbd dup invs o oT oTe proj xb x3"
FFN_SEMS = ("stats moments centred lnT lnTe mm gmax eq cand first ind gsub gexp gsum gtop q kw ks vw vs vtop krep T "
            "qT kbd dup masked y")


def scores_pe(nc, pe, S, i, psS, qT, kbd):
    for b in range(2):
        for c in range(NC):
            last = nc.tensor.matmul(psS[b * SQ:(b + 1) * SQ, c, :], qT[:, c, b * SQ:(b + 1) * SQ], kbd(c, b),
                                    start=True, stop=True)
    last.then_inc(S.smm, 1)


def weigh_pe(nc, pe, T, S, i, psK, psO, prob, pT, vbd):
    pe.wait_ge(S.exp, at(i, 1, 1))
    pe.wait_ge(S.pTe, at(i, 1, 0))
    for m in range(HS // 2):
        last = nc.tensor.transpose(psK[:, m // 4, m % 4 * P:(m % 4 + 1) * P], prob[:, m * P:(m + 1) * P], T.ident[:, :])
    last.then_inc(S.pT, 1)
    pe.wait_ge(S.pTe, at(i, 1, 1))
    pe.wait_ge(S.vbd, at(i, 1, 1))
    for b in range(2):
        for m in range(HS // 2):
            last = nc.tensor.matmul(psO[b * SQ:(b + 1) * SQ, 0, m * 2 * DS:(m + 1) * 2 * DS],
                                    pT[:, m, b * SQ:(b + 1) * SQ], vbd(b, m), start=True, stop=True)
    last.then_inc(S.pv, 1)


def softmax_dve(nc, dve, S, i, scores, shifted, st):
    nc.vector.tensor_reduce(st[:, 0, :], scores.rearrange("p (h k) -> p h k", k=SQ), AX.X, ALU.max).then_inc(S.smax, 1)
    dve.wait_ge(S.smax, at(i, 1, 1))
    dve.wait_ge(S.pT, at(i, 1, 0))
    nc.vector.tensor_tensor(shifted.rearrange("p (h k) -> p h k", k=SQ), scores.rearrange("p (h k) -> p h k", k=SQ),
                            over(st[:, 0, :], SQ), ALU.subtract).then_inc(S.sub, 1)


def softmax_sum_dve(nc, dve, S, i, prob, st):
    dve.wait_ge(S.exp, at(i, 1, 1))
    nc.vector.tensor_reduce(st[:, 1, :], prob.rearrange("p (h k) -> p h k", k=SQ), AX.X, ALU.add).then_inc(S.total, 1)
    dve.wait_ge(S.total, at(i, 1, 1))
    nc.vector.reciprocal(st[:, 2, :], st[:, 1, :]).then_inc(S.inv, 1)


def self_attentions(nc, T, psum, dram):
    psT, psK, psS, psO, psM = psum
    with ExitStack() as ctx:
        def sb(name, shape, dt=F32):
            return ctx.enter_context(nc.sbuf_tensor(f"s_{name}", shape, dt))

        wout, bout = sb("wout", [P, WC, DIM]), sb("bout", [P, DIM])
        wgate, wgT = sb("wgate", [HS, DIM]), sb("wgT", [P, WC, HS])
        wqkv, wT = sb("wqkv", [P, 3 * WC, DIM]), sb("wT", [P, WC, 3 * DIM])
        am, sc = sb("am", [P, 3]), sb("sc", [P, 4, 3])
        mask8, mask2 = sb("mask8", [P, HH]), sb("mask2", [P, 2])
        sel, selb = sb("sel", [P, 2, 2, SQ]), sb("selb", [P, 2, 2, SQ], BF16)
        maskc, iota_i, iota = sb("maskc", [P, SQ]), sb("iota_i", [P, HS], I32), sb("iota", [P, HS])
        u, e, r8 = sb("u", [P, 3 * DIM]), sb("e", [P, 3 * DIM]), sb("r8", [P, 3 * DIM], BF16)
        q8T, k8bd = sb("q8T", [P, NC, P], BF16), sb("k8bd", [P, NC, 2, HH, SQ], BF16)
        prob, pT = sb("prob", [P, HS * SQ]), sb("pT", [P, HS // 2, P])
        vbd, vbd2 = sb("vbd", [P, 2, HS // 2, 2, DS]), sb("vbd2", [P, 2, 2, DS])
        st, o, oT = sb("st", [P, 4, HS]), sb("o", [P, DIM]), sb("oT", [P, WC, P])
        xb, x3 = sb("xb", [P, DIM]), sb("x3", [P, DIM])
        stats, mv, lx = sb("stats", [P, 6]), sb("mv", [P, 2]), sb("lx", [P, 5, 1])
        xn, xT = sb("xn", [P, WC, P]), sb("xT", [P, WC, P])
        gt, gs = sb("gt", [P, 5, HS]), sb("gs", [P, 4])
        q2, q2T = sb("q2", [P, DIM]), sb("q2T", [P, NC, P])
        kw, vw, ks = sb("kw", [P, DIM]), sb("vw", [P, DIM]), sb("ks", [P, 3, DS])
        krep, k2bd = sb("krep", [P, HH, DS]), sb("k2bd", [P, 2, HH, SQ])
        prob2, y = sb("prob2", [P, HS * SQ]), sb("y", [P, DIM])
        W, A, AS, G, GS, L = primed(nc, ctx, ("ws", "wout bout wgate wqkv gT gTe wT wTe m8 m2 sel causal iota iotaf selb am amall sc stored passed"),
                                    ("att", ATT_SEMS), ("attsm", SM_SEMS), ("ffn", FFN_SEMS), ("ffnsm", SM_SEMS), ("ffnln", ROOT))
        stored = W.stored
        bf = psT[:, :].bitcast(BF16)
        block = ctx.enter_context(nc.Block())
        s_flat = psS[:, :, :].rearrange("p a n -> p (a n)")

        @block.sync
        def _(sp):
            sp.dma_start(wqkv[:, :, :], dram["L0_ffn_W_qkv"].rearrange("(k p) n -> p k n", p=P)).then_inc(W.wqkv, 16)
            sp.dma_start(wgate[:, :], dram["L0_ffn_W_gate"]).then_inc(W.wgate, 16)
            sp.dma_start(wout[:, :, :], dram["L0_attn_W_out"].rearrange("(k p) n -> p k n", p=P)).then_inc(W.wout, 16)
            sp.dma_start(bout[:, :], dram["L0_attn_b_out"].rearrange("(a n) -> a n", a=1).broadcast_to([P, DIM])).then_inc(W.bout, 16)
            out = dram["out"].rearrange("b q c -> (b q) c").rearrange("(n p) c -> n p c", p=P)
            with sp.Fori(0, NPAIR) as i:
                sp.wait_ge(G.y, at(i, 2, 2))
                sp.dma_start(out[bass.ds(i, 1), :, :].rearrange("n p c -> (n p) c"), y[:, :]).then_inc(stored, 16)
                sp.wait_ge(stored, 16 * i + 16)
                alone(sp, W.passed)

        @block.gpsimd
        def _(pool):
            for m, width, sem in ((mask8, DS, W.m8), (mask2, SQ, W.m2)):
                n = P // width
                nc.gpsimd.memset(m[:, :], 1.0).then_inc(sem, 1)
                pool.wait_ge(sem, 1)
                nc.gpsimd.affine_select(out=m[:, :], in_=m[:, :], compare_op=ALU.is_ge, fill=0.0, base=0,
                                        pattern=[[-width, n]], channel_multiplier=1).then_inc(sem, 1)
                pool.wait_ge(sem, 2)
                nc.gpsimd.affine_select(out=m[:, :], in_=m[:, :], compare_op=ALU.is_ge, fill=0.0, base=width - 1,
                                        pattern=[[width, n]], channel_multiplier=-1).then_inc(sem, 1)
            nc.gpsimd.memset(sel[:, :, :, :], 0.0).then_inc(W.sel, 1)
            pool.wait_ge(W.sel, 1)
            nc.gpsimd.affine_select(out=sel[:, :, :, :], in_=sel[:, :, :, :], compare_op=ALU.not_equal, fill=1.0, base=0,
                                    pattern=[[-SQ, 2], [0, 2], [-1, SQ]], channel_multiplier=1).then_inc(W.sel, 1)
            nc.gpsimd.memset(maskc[:, :], 0.0).then_inc(W.causal, 1)
            pool.wait_ge(W.causal, 1)
            for b in range(2):
                rows = slice(b * SQ, (b + 1) * SQ)
                pool.wait_ge(W.causal, b + 1)
                nc.gpsimd.affine_select(out=maskc[rows, :], in_=maskc[rows, :], compare_op=ALU.is_ge, fill=-FAR, base=0,
                                        pattern=[[-1, SQ]], channel_multiplier=1).then_inc(W.causal, 1)
            pool.wait_ge(W.causal, 3)
            nc.gpsimd.iota(iota_i[:, :], pattern=[[1, HS]], base=-HS, channel_multiplier=0).then_inc(W.iota, 1)
            pool.wait_ge(W.am, 1)
            nc.gpsimd.partition_all_reduce(sc[:, 0, :], am[:, :], P, ABSMAX).then_inc(W.amall, 1)

        @block.tensor
        def _(pe):
            pe.wait_ge(W.wgate, 16)
            for k in range(WC):
                last = nc.tensor.transpose(psT[:, k * HS:(k + 1) * HS], wgate[:, k * P:(k + 1) * P], T.ident[0:HS, 0:HS])
            last.then_inc(W.gT, 1)
            pe.wait_ge(W.wqkv, 16)
            for k in range(WC):
                for f in range(3 * WC):
                    bank, n = (psK, psS)[k], f
                    last = nc.tensor.transpose(bank[:, n // 4, n % 4 * P:(n % 4 + 1) * P], wqkv[:, f, k * P:(k + 1) * P], T.ident[:, :])
                last.then_inc(W.wT, 1)
            pe.wait_ge(W.gTe, 1)
            pe.wait_ge(W.wTe, 2 * WC)
            pe.wait_ge(W.wout, 16)
            pe.wait_ge(W.selb, 1)
            with pe.Fori(0, NPAIR) as i:
                pe.wait_ge(A.q8, at(i, 1, 1))
                pe.wait_ge(G.kbd, at(i, 1, 0))
                for n in range(2 * NC):
                    last = nc.tensor.transpose(bf[:, n * P:(n + 1) * P], r8[:, n * P:(n + 1) * P], T.identb[:, :])
                last.then_inc(A.T, 1)
                pe.wait_ge(GS.vbd, at(i, 1, 0))
                for b in range(2):
                    last = nc.tensor.matmul(psM[:, b * DIM:(b + 1) * DIM], selb[:, b, :, :].rearrange("p c k -> p (c k)"),
                                            r8[:, 2 * DIM:3 * DIM], start=True, stop=True)
                last.then_inc(A.dup, 1)
                pe.wait_ge(A.qT, at(i, 1, 1))
                pe.wait_ge(A.kbd, at(i, NC, NC))
                pe.wait_ge(GS.sub, at(i, 1, 0))
                scores_pe(nc, pe, AS, i, psS, q8T, lambda c, b: k8bd[:, c, b, :, :].rearrange("p h k -> p (h k)"))
                weigh_pe(nc, pe, T, AS, i, psK, psO, prob, pT, lambda b, m: vbd[:, b, m, :, :].rearrange("p h d -> p (h d)"))
                pe.wait_ge(A.o, at(i, 1, 1))
                for k in range(WC):
                    last = nc.tensor.transpose(psT[:, k * P:(k + 1) * P], o[:, k * P:(k + 1) * P], T.ident[:, :])
                last.then_inc(A.oT, 1)
                pe.wait_ge(A.oTe, at(i, 1, 1))
                for k in range(WC):
                    last = nc.tensor.matmul(psO[:, 1, 0:DIM], oT[:, k, :], wout[:, k, :], start=(k == 0), stop=(k == WC - 1))
                last.then_inc(A.proj, 1)
                pe.wait_ge(G.centred, at(i, 1, 1))
                for k in range(WC):
                    last = nc.tensor.transpose(psT[:, k * P:(k + 1) * P], xn[:, k, :], T.ident[:, :])
                last.then_inc(G.lnT, 1)
                pe.wait_ge(G.lnTe, at(i, 1, 1))
                for out, w in ((psM[:, 0:HS], lambda k: wgT[:, k, :]), (psS[:, 0, :], lambda k: wT[:, k, 0:2 * DIM]),
                               (psS[:, 1, 0:DIM], lambda k: wT[:, k, 2 * DIM:3 * DIM])):
                    for k in range(WC):
                        last = nc.tensor.matmul(out, xT[:, k, :], w(k), start=(k == 0), stop=(k == WC - 1))
                    last.then_inc(G.mm, 1)
                pe.wait_ge(G.krep, at(i, 1, 1))
                pe.wait_ge(G.q, at(i, 1, 1))
                for n in range(NC):
                    nc.tensor.transpose(psT[:, n * P:(n + 1) * P], q2[:, n * P:(n + 1) * P], T.ident[:, :])
                nc.tensor.transpose(psT[:, NC * P:(NC + 1) * P], krep[:, :, :].rearrange("p h d -> p (h d)"), T.ident[:, :]).then_inc(G.T, 1)
                pe.wait_ge(G.vtop, at(i, 1, 1))
                for b in range(2):
                    last = nc.tensor.matmul(psM[:, 2 * HS + b * DS:2 * HS + (b + 1) * DS], sel[:, b, :, :].rearrange("p c k -> p (c k)"),
                                            ks[:, 2, :], start=True, stop=True)
                last.then_inc(G.dup, 1)
                pe.wait_ge(G.qT, at(i, 1, 1))
                pe.wait_ge(G.kbd, at(i, 1, 1))
                pe.wait_ge(G.vw, at(i, 1, 1))
                scores_pe(nc, pe, GS, i, psS, q2T, lambda c, b: k2bd[:, b, :, :].rearrange("p h k -> p (h k)"))
                weigh_pe(nc, pe, T, GS, i, psK, psO, prob2, pT, lambda b, m: vbd2[:, b, :, :].rearrange("p h d -> p (h d)"))

        @block.scalar
        def _(act):
            act.wait_ge(W.gT, 1)
            nc.scalar.activation(wgT[:, :, :], psT[:, 0:WC * HS].rearrange("p (k h) -> p k h", k=WC), ACT.Copy).then_inc(W.gTe, 1)
            for k in range(WC):
                act.wait_ge(W.wT, k + 1)
                bank = (psK, psS)[k]
                nc.scalar.activation(wT[:, k, 0:BANK], bank[:, 0, :], ACT.Copy).then_inc(W.wTe, 1)
                nc.scalar.activation(wT[:, k, BANK:3 * DIM], bank[:, 1, 0:3 * DIM - BANK], ACT.Copy).then_inc(W.wTe, 1)
            nc.scalar.preload_act_table_set(LN_EXP)
            act.wait_ge(W.sc, 5)
            with act.Fori(0, NPAIR) as i:
                act.wait_ge(A.T, at(i, 1, 1))
                nc.scalar.activation(q8T[:, :, :].rearrange("p c n -> p (c n)"), bf[:, 0:NC * P], ACT.Copy).then_inc(A.qT, 1)
                act.wait_ge(AS.sub, at(i, 1, 1))
                nc.scalar.activation(prob[:, :], prob[:, :], ACT.Exp, scale=sc[:, 3, 0:1]).then_inc(AS.exp, 1)
                act.wait_ge(AS.pT, at(i, 1, 1))
                nc.scalar.activation(pT[:, :, :].rearrange("p m n -> p (m n)"), psK[:, :, :].rearrange("p a n -> p (a n)"), ACT.Copy).then_inc(AS.pTe, 1)
                act.wait_ge(A.oT, at(i, 1, 1))
                nc.scalar.activation(oT[:, :, :].rearrange("p k n -> p (k n)"), psT[:, 0:DIM], ACT.Copy).then_inc(A.oTe, 1)
                inverse_root_guess(nc, act, L, i, lx[:, 1, :], lx[:, 2, :], lx[:, 0, :])
                act.wait_ge(G.lnT, at(i, 1, 1))
                nc.scalar.activation(xT[:, :, :].rearrange("p k n -> p (k n)"), psT[:, 0:DIM], ACT.Copy).then_inc(G.lnTe, 1)
                act.wait_ge(G.mm, at(i, 3, 2))
                nc.scalar.activation(q2[:, :], psS[:, 0, 0:DIM], ACT.Copy).then_inc(G.q, 1)
                act.wait_ge(G.gsub, at(i, 1, 1))
                nc.scalar.activation(gt[:, 4, :], gt[:, 3, :], ACT.Exp).then_inc(G.gexp, 1)
                act.wait_ge(G.T, at(i, 1, 1))
                nc.scalar.activation(q2T[:, :, :].rearrange("p k n -> p (k n)"), psT[:, 0:DIM], ACT.Copy).then_inc(G.qT, 1)
                act.wait_ge(GS.sub, at(i, 1, 1))
                nc.scalar.activation(prob2[:, :], prob2[:, :], ACT.Exp, scale=1.0 / np.sqrt(DS)).then_inc(GS.exp, 1)
                act.wait_ge(GS.pT, at(i, 1, 1))
                nc.scalar.activation(pT[:, :, :].rearrange("p m n -> p (m n)"), psK[:, :, :].rearrange("p a n -> p (a n)"), ACT.Copy).then_inc(GS.pTe, 1)

        @block.vector
        def _(dve):
            nc.vector.tensor_reduce(am[:, :], T.amax[:, :, :].rearrange("p n g -> p g n"), AX.X, ALU.max).then_inc(W.am, 1)
            dve.wait_ge(W.sel, 2)
            nc.vector.tensor_copy(selb[:, :, :, :], sel[:, :, :, :]).then_inc(W.selb, 1)
            dve.wait_ge(W.iota, 1)
            nc.vector.tensor_copy(iota[:, :], iota_i[:, :]).then_inc(W.iotaf, 1)
            dve.wait_ge(W.amall, 1)
            nc.vector.tensor_scalar(sc[:, 1, :], sc[:, 0, :], 1.0 / FP8_MAX, None, ALU.mult).then_inc(W.sc, 1)
            dve.wait_ge(W.sc, 1)
            nc.vector.reciprocal(sc[:, 2, :], sc[:, 1, :]).then_inc(W.sc, 1)
            nc.vector.tensor_tensor(sc[:, 3, 1:2], sc[:, 1, 0:1], sc[:, 1, 1:2], ALU.mult).then_inc(W.sc, 1)
            dve.wait_ge(W.sc, 3)
            nc.vector.tensor_scalar(sc[:, 3, 0:1], sc[:, 3, 1:2], float(1.0 / np.sqrt(DS)), None, ALU.mult).then_inc(W.sc, 1)
            dve.wait_ge(W.sc, 4)
            nc.vector.tensor_copy(sc[:, 3, 2:3], sc[:, 1, 2:3]).then_inc(W.sc, 1)
            dve.wait_ge(W.m8, 3)
            dve.wait_ge(W.m2, 3)
            dve.wait_ge(W.causal, 3)
            dve.wait_ge(W.iotaf, 1)
            dve.wait_ge(W.bout, 16)
            dve.wait_ge(W.sc, 5)
            with dve.Fori(0, NPAIR) as i:
                raw = T.qkv[:, bass.ds(i, 1), :].rearrange("p n (g m) -> p (n g) m", g=3)
                nc.vector.tensor_tensor(u[:, :].rearrange("p (g m) -> p g m", g=3), raw, over(sc[:, 2, :], DIM), ALU.mult).then_inc(A.u, 1)
                dve.wait_ge(A.u, at(i, 1, 1))
                nc.vector.tensor_scalar(e[:, :].bitcast(I32), u[:, :].bitcast(I32), 0x7F800000, None, ALU.bitwise_and).then_inc(A.expo, 1)
                dve.wait_ge(A.expo, at(i, 1, 1))
                nc.vector.tensor_scalar(e[:, :], e[:, :], 2.0 ** -6, 1.5 * 2.0 ** 20, ALU.max, ALU.mult).then_inc(A.magic, 1)
                dve.wait_ge(A.magic, at(i, 1, 1))
                nc.vector.tensor_tensor(u[:, :], u[:, :], e[:, :], ALU.add).then_inc(A.sum, 1)
                dve.wait_ge(A.sum, at(i, 1, 1))
                nc.vector.tensor_tensor(r8[:, :], u[:, :], e[:, :], ALU.subtract).then_inc(A.q8, 1)
                x2 = T.xs[:, bass.ds(i, 1), :].rearrange("p n c -> p (n c)")
                nc.vector.tensor_tensor(xb[:, :], x2, bout[:, :], ALU.add).then_inc(A.xb, 1)
                dve.wait_ge(A.qT, at(i, 1, 1))
                for c in range(NC):
                    k8 = bf[:, (NC + c) * P:(NC + c + 1) * P].rearrange("p (b k) -> p b k", b=2).unsqueeze(2).broadcast_to([P, 2, HH, SQ])
                    m8 = mask8[:, :].unsqueeze(1).unsqueeze(3).broadcast_to([P, 2, HH, SQ])
                    nc.vector.tensor_tensor(k8bd[:, c, :, :, :], k8, m8, ALU.mult).then_inc(A.kbd, 1)
                dve.wait_ge(A.dup, at(i, 1, 1))
                for b in range(2):
                    last = nc.vector.tensor_tensor(vbd[:, b, :, :, :],
                                                   psM[:, b * DIM:(b + 1) * DIM].rearrange("p (m h d) -> p m h d", h=2, d=DS),
                                                   mask2[:, :].unsqueeze(1).unsqueeze(3).broadcast_to([P, HS // 2, 2, DS]), ALU.mult)
                last.then_inc(AS.vbd, 1)
                dve.wait_ge(AS.smm, at(i, 1, 1))
                softmax_dve(nc, dve, AS, i, s_flat, prob[:, :], st)
                softmax_sum_dve(nc, dve, AS, i, prob[:, :], st)
                dve.wait_ge(AS.inv, at(i, 1, 1))
                nc.vector.tensor_scalar(st[:, 3, :], st[:, 2, :], sc[:, 3, 2:3], None, ALU.mult).then_inc(A.invs, 1)
                dve.wait_ge(A.invs, at(i, 1, 1))
                dve.wait_ge(AS.pv, at(i, 1, 1))
                nc.vector.tensor_tensor(o[:, :].rearrange("p (h d) -> p h d", d=DS), psO[:, 0, 0:DIM].rearrange("p (h d) -> p h d", d=DS),
                                        over(st[:, 3, :], DS), ALU.mult).then_inc(A.o, 1)
                dve.wait_ge(A.proj, at(i, 1, 1))
                nc.vector.tensor_tensor(x3[:, :], psO[:, 1, 0:DIM], xb[:, :], ALU.add).then_inc(A.x3, 1)
                dve.wait_ge(A.x3, at(i, 1, 1))
                nc.vector.bn_stats(stats[:, :], x3[:, :]).then_inc(G.stats, 1)
                dve.wait_ge(G.stats, at(i, 1, 1))
                alone(dve, W.passed)
                nc.vector.bn_aggr(mv[:, :], stats[:, :]).then_inc(G.moments, 1)
                dve.wait_ge(G.moments, at(i, 1, 1))
                inverse_root_start(nc, dve, L.x, lx[:, 0, :], mv[:, 1:2], 1)
                inverse_root_end(nc, dve, L, i, lx[:, 2, :], lx[:, 3, :], lx[:, 0, :], lx[:, 4, :])
                dve.wait_ge(L.root, at(i, 1, 1))
                nc.vector.tensor_scalar(xn[:, :, :].rearrange("p k n -> p (k n)"), x3[:, :], mv[:, 0:1], lx[:, 4, :],
                                        ALU.subtract, ALU.mult).then_inc(G.centred, 1)
                dve.wait_ge(G.mm, at(i, 3, 1))
                nc.vector.tensor_reduce(gs[:, 0:1], psM[:, 0:HS], AX.X, ALU.max).then_inc(G.gmax, 1)
                dve.wait_ge(G.gmax, at(i, 1, 1))
                nc.vector.tensor_scalar(gt[:, 3, :], psM[:, 0:HS], gs[:, 0:1], None, ALU.subtract).then_inc(G.gsub, 1)
                nc.vector.tensor_scalar(gt[:, 0, :], psM[:, 0:HS], gs[:, 0:1], None, ALU.is_ge).then_inc(G.eq, 1)
                dve.wait_ge(G.eq, at(i, 1, 1))
                nc.vector.tensor_tensor(gt[:, 1, :], gt[:, 0, :], iota[:, :], ALU.mult).then_inc(G.cand, 1)
                dve.wait_ge(G.cand, at(i, 1, 1))
                nc.vector.tensor_reduce(gs[:, 1:2], gt[:, 1, :], AX.X, ALU.min).then_inc(G.first, 1)
                dve.wait_ge(G.first, at(i, 1, 1))
                nc.vector.tensor_scalar(gt[:, 2, :], iota[:, :], gs[:, 1:2], None, ALU.is_equal).then_inc(G.ind, 1)
                dve.wait_ge(G.ind, at(i, 1, 1))
                dve.wait_ge(G.q, at(i, 1, 1))
                nc.vector.tensor_tensor(kw[:, :].rearrange("p (h d) -> p h d", d=DS), psS[:, 0, DIM:2 * DIM].rearrange("p (h d) -> p h d", d=DS),
                                        over(gt[:, 2, :], DS), ALU.mult).then_inc(G.kw, 1)
                dve.wait_ge(G.mm, at(i, 3, 3))
                nc.vector.tensor_tensor(vw[:, :].rearrange("p (h d) -> p h d", d=DS), psS[:, 1, 0:DIM].rearrange("p (h d) -> p h d", d=DS),
                                        over(gt[:, 2, :], DS), ALU.mult).then_inc(G.vw, 1)
                dve.wait_ge(G.kw, at(i, 1, 1))
                nc.vector.tensor_reduce(ks[:, 0, :], kw[:, :].rearrange("p (h d) -> p d h", d=DS), AX.X, ALU.add).then_inc(G.ks, 1)
                dve.wait_ge(G.ks, at(i, 1, 1))
                nc.vector.tensor_copy(krep[:, :, :], ks[:, 0, :].unsqueeze(1).broadcast_to([P, HH, DS])).then_inc(G.krep, 1)
                dve.wait_ge(G.vw, at(i, 1, 1))
                nc.vector.tensor_reduce(ks[:, 1, :], vw[:, :].rearrange("p (h d) -> p d h", d=DS), AX.X, ALU.add).then_inc(G.vs, 1)
                dve.wait_ge(G.gexp, at(i, 1, 1))
                nc.vector.tensor_reduce(gs[:, 2:3], gt[:, 4, :], AX.X, ALU.add).then_inc(G.gsum, 1)
                dve.wait_ge(G.gsum, at(i, 1, 1))
                nc.vector.reciprocal(gs[:, 3:4], gs[:, 2:3]).then_inc(G.gtop, 1)
                dve.wait_ge(G.gtop, at(i, 1, 1))
                dve.wait_ge(G.vs, at(i, 1, 1))
                nc.vector.tensor_scalar(ks[:, 2, :], ks[:, 1, :], gs[:, 3:4], None, ALU.mult).then_inc(G.vtop, 1)
                dve.wait_ge(G.qT, at(i, 1, 1))
                k2 = psT[:, NC * P:(NC + 1) * P].rearrange("p (b k) -> p b k", b=2).unsqueeze(2).broadcast_to([P, 2, HH, SQ])
                nc.vector.tensor_tensor(k2bd[:, :, :, :], k2, mask8[:, :].unsqueeze(1).unsqueeze(3).broadcast_to([P, 2, HH, SQ]), ALU.mult).then_inc(G.kbd, 1)
                dve.wait_ge(G.dup, at(i, 1, 1))
                nc.vector.tensor_tensor(vbd2[:, :, :, :], psM[:, 2 * HS:2 * HS + 2 * DS].rearrange("p (b d) -> p b d", b=2).unsqueeze(2).broadcast_to([P, 2, 2, DS]),
                                        mask2[:, :].unsqueeze(1).unsqueeze(3).broadcast_to([P, 2, 2, DS]), ALU.mult).then_inc(GS.vbd, 1)
                dve.wait_ge(GS.smm, at(i, 1, 1))
                dve.wait_ge(GS.pT, at(i, 1, 0))
                nc.vector.tensor_tensor(prob2[:, :].rearrange("p (h k) -> p h k", k=SQ), s_flat.rearrange("p (h k) -> p h k", k=SQ),
                                        maskc[:, :].unsqueeze(1).broadcast_to([P, HS, SQ]), ALU.add).then_inc(G.masked, 1)
                dve.wait_ge(G.masked, at(i, 1, 1))
                softmax_dve(nc, dve, GS, i, prob2[:, :], prob2[:, :], st)
                softmax_sum_dve(nc, dve, GS, i, prob2[:, :], st)
                dve.wait_ge(GS.inv, at(i, 1, 1))
                dve.wait_ge(GS.pv, at(i, 1, 1))
                dve.wait_ge(stored, 16 * i)
                nc.vector.tensor_tensor(y[:, :].rearrange("p (h d) -> p h d", d=DS), psO[:, 0, 0:DIM].rearrange("p (h d) -> p h d", d=DS),
                                        over(st[:, 2, :], DS), ALU.mult).then_inc(G.y, 1)
                dve.wait_ge(G.y, at(i, 2, 1))
                nc.vector.tensor_tensor(y[:, :], y[:, :], x3[:, :], ALU.add).then_inc(G.y, 1)


def build(nc, dram):
    with ExitStack() as ctx:
        def sb(name, shape, dt=F32):
            return ctx.enter_context(nc.sbuf_tensor(name, shape, dt))

        def pb(name, banks):
            return ctx.enter_context(nc.psum_tensor(name, [P, banks, BANK] if banks > 1 else [P, BANK], F32))

        psum = pb("psT", 1), pb("psK", 2), pb("psS", 2), pb("psO", 2), pb("psM", 1)
        T = Shared()
        T.ident, T.identb = sb("ident", [P, P]), sb("identb", [P, P], BF16)
        T.ones, T.zero, T.shift, T.gcol = sb("ones", [P, 1]), sb("zero", [P, 1]), sb("shift", [P, 1]), sb("gcol", [P, 2])
        T.xs, T.rden, T.amax = sb("xs", [P, NPAIR, DIM]), sb("rden", [P, NPAIR, H]), sb("amax", [P, NPAIR, 3])
        with ExitStack() as crossing:
            T.big = crossing.enter_context(nc.sbuf_tensor("big", [P, NPAIR * 2 * HQ], F32))
            T.queries = T.big[:, :].rearrange("p (n b h q) -> p n b h q", n=NPAIR, b=2, q=SQ)
            with ExitStack() as keys:
                T.wkh = keys.enter_context(nc.sbuf_tensor("wkh", [P, INNER], F32R))
                T.wkl = keys.enter_context(nc.sbuf_tensor("wkl", [P, INNER], F32R))
                setup(nc, T, psum, dram)
                queries(nc, T, psum, dram)
                cross_attention(nc, T, psum, dram)
            T.qkv = crossing.enter_context(nc.sbuf_tensor("qkv", [P, NPAIR, 3 * DIM], F32))
            project(nc, T, psum, dram)
            self_attentions(nc, T, psum, dram)


_INS = ["x", "ctx_1024", "L0_xattn_Wq", "L0_xattn_Wk", "L0_xattn_Wv", "L0_xattn_Wo", "L0_xattn_gq", "L0_xattn_gk",
        "L0_attn_W_qkv", "L0_attn_W_out", "L0_attn_b_out", "L0_ffn_W_gate", "L0_ffn_W_qkv"]


def kernel(**inputs):
    import concourse.bacc as bacc
    from concourse.bass_utils import run_bass_kernel_spmd

    nc = bacc.Bacc("TRN2", target_bir_lowering=False, num_devices=1)
    arrays, dram = {}, {}
    for name in _INS:
        a = np.ascontiguousarray(inputs[name])
        arrays[f"in_{name}"] = a
        dram[name] = nc.dram_tensor(f"in_{name}", a.shape, mybir.dt.from_np(a.dtype), kind="ExternalInput").ap()
    dram["out"] = nc.dram_tensor("out", (B, SQ, DIM), F32, kind="ExternalOutput").ap()
    build(nc, dram)
    result = run_bass_kernel_spmd(nc, [arrays], core_ids=[0])
    return result.results[0]["out"]
```

```python
from collections import namedtuple
from contextlib import ExitStack

import concourse.bass as bass
import numpy as np
from concourse import mybir
from concourse.alu_op_type import AluOpType as ALU

F32 = mybir.dt.float32
F32R = mybir.dt.float32r
BF16 = mybir.dt.bfloat16
I32 = mybir.dt.int32
ACT = mybir.ActivationFunctionType
AX = mybir.AxisListType
ABSMAX = bass.bass_isa.ReduceOp.absmax

B, SQ, DIM = 16, 64, 256
SKV, CD = 1601, 128
H, D = 16, 128
INNER = H * D
HS, DS = 16, 16
P = 128
WC = DIM // P
NPAIR = B // 2
HQ = H * SQ
NT = -(-SKV // P)
ROWS = -(-SKV // NT)
FULL = SKV // NT
REST = SKV - FULL * NT
TP = 2 * NT
BANK = 512
HB = BANK // D
KC = INNER // BANK
GROUPS = NPAIR * P // BANK
GP = BANK // P
PW = BANK // DIM
EPS = 1e-5
SCALE = 1.0 / np.sqrt(D)
LIMIT = 60.0
FP8_MAX = 448.0
FAR = 1e30
CREDIT = 64
LN_EXP = "natural_log_exp_and_others"


def rows_of(n):
    return ROWS if n % NT < REST else FULL


def ring(length, slots, apart):
    whole = next(n for n in range(length // slots, -1, -1) if (length - n * slots) % apart == 0)
    return list(range(slots)) * whole + list(range(apart)) * ((length - whole * slots) // apart)


LAG = 9
CT_SLOTS = 5
CT_SLOT = ring(TP, CT_SLOTS, 4)


PIECES = [slice(NT * n // 4, NT * (n + 1) // 4) for n in range(4)]


CONTEXT_HIGH, CONTEXT_LOW = (2, 3, 8, 9), (4, 5, 10, 11)


def ct_before(t):
    return next(k for k in range(1, TP) if CT_SLOT[(t - k) % TP] == CT_SLOT[t % TP])


def at(i, per, k):
    return per * i + (CREDIT + k)


class Shared:
    pass


def semaphores(nc, ctx, tag, names):
    return namedtuple(tag, names)(*(ctx.enter_context(nc.semaphore(f"{tag}_{n}")) for n in names.split()))


def alone(eng, sem):
    eng.sem_inc(sem, 1)


def over(ap, n):
    return ap.unsqueeze(len(ap.shape)).broadcast_to([*ap.shape, n])


def inverse_root_start(nc, dve, sem, x, total, n):
    nc.vector.tensor_scalar(x, total, 1.0 / n, EPS, ALU.mult, ALU.add).then_inc(sem, 1)


def inverse_root_guess(nc, act, S, i, log, y, x):
    act.wait_ge(S.x, at(i, 1, 1))
    nc.scalar.activation(log, x, ACT.Ln).then_inc(S.log, 1)
    act.wait_ge(S.log, at(i, 1, 1))
    nc.scalar.activation(y, log, ACT.Exp, scale=-0.5).then_inc(S.guess, 1)


def inverse_root_end(nc, dve, S, i, y, u, x, out):
    dve.wait_ge(S.guess, at(i, 1, 1))
    nc.vector.scalar_tensor_tensor(u, y, -0.5, y, ALU.mult, ALU.mult).then_inc(S.newton, 1)
    dve.wait_ge(S.newton, at(i, 2, 1))
    nc.vector.tensor_tensor(u, u, x, ALU.mult).then_inc(S.newton, 1)
    dve.wait_ge(S.newton, at(i, 2, 2))
    nc.vector.scalar_tensor_tensor(out, u, 1.5, y, ALU.add, ALU.mult).then_inc(S.root, 1)


ROOT = "x log guess newton root"



def primed(nc, ctx, plain, *loops):
    zero, made = semaphores(nc, ctx, *plain), [semaphores(nc, ctx, *group) for group in loops]
    sems = [(sem, 0) for sem in zero] + [(sem, CREDIT) for group in made for sem in group]

    def prime(eng, first):
        for sem, value in sems[first::5]:
            eng.sem_clear(sem)
            if value:
                eng.sem_inc(sem, value)

    with nc.Block() as block:
        @block.sync
        def _(sp):
            prime(sp, 0)

        @block.scalar
        def _(act):
            prime(act, 1)

        @block.vector
        def _(dve):
            prime(dve, 2)

        @block.gpsimd
        def _(pool):
            prime(pool, 3)

        @block.tensor
        def _(pe):
            prime(pe, 4)

    return (zero, *made)



PREP_SEMS = ("x gains wk wq0 wq1 wq2 wq3 consts gprod gmax made stats moments centred lnT lnTh lnTl wkT wkTh wkTl wqh wql "
             "wkh wkl")
Q_SLOTS = 3
ITEM_SEMS = "q square qgh qgl total log y half newton root qw out"


def queries(nc, T, psum, dram):
    psT, psK, psS, psO, psM = psum
    with ExitStack() as ctx:
        def sb(name, shape, dt=F32):
            return ctx.enter_context(nc.sbuf_tensor(f"q_{name}", shape, dt))

        g2, gmax, eps = sb("g2", [P, 2]), sb("gmax", [P, 2]), sb("eps", [P, 1])
        wk, wq = sb("wk", [P, INNER]), sb("wq", [P, WC, INNER])
        wqh, wql = sb("wqh", [P, WC, INNER], F32R), sb("wql", [P, WC, INNER], F32R)
        wkTh, wkTl = sb("wkTh", [P, H, CD], F32R), sb("wkTl", [P, H, CD], F32R)
        stats, mv = sb("stats", [P, NPAIR, 6]), sb("mv", [P, NPAIR, 2])
        lx = sb("lx", [P, 5, NPAIR])
        xTh, xTl = sb("xTh", [P, WC, NPAIR * P], F32R), sb("xTl", [P, WC, NPAIR * P], F32R)
        square, log, half = sb("square", [P, 2, BANK]), sb("log", [P, BANK]), sb("half", [P, BANK])
        y, scaled, root = sb("y", [P, 2, BANK]), sb("scaled", [P, BANK]), sb("root", [P, BANK])
        qgh, qgl = sb("qgh", [P, Q_SLOTS, BANK], F32R), sb("qgl", [P, Q_SLOTS, BANK], F32R)
        S, L = primed(nc, ctx, ("query", PREP_SEMS + " " + ITEM_SEMS), ("queryln", ROOT))
        wq_there = (S.wq0, S.wq1, S.wq2, S.wq3)
        items = [(h, g) for h in range(H) for g in range(GROUPS)]
        turned = [(psK, 0), (psK, 1), (psS, 0), (psS, 1)]
        block = ctx.enter_context(nc.Block())

        def xn_of(pair):
            return y[:, pair % 2, 0:DIM]

        def quad(q):
            return slice(q * BANK, (q + 1) * BANK)

        def out(n):
            h, g = items[n]
            return T.queries[:, g * GP:(g + 1) * GP, :, h, :].rearrange("p n b q -> p (n b) q")

        def steps(step):
            for n in range(len(items) + 2):
                step(n if n < len(items) else None, n - 1 if 0 <= n - 1 < len(items) else None, n - 2 if n >= 2 else None)

        @block.sync
        def _(sp):
            sp.dma_start(T.xs[:, :, :], dram["x"].rearrange("b q c -> (b q) c").rearrange("(n p) c -> p n c", p=P)).then_inc(S.x, 16)
            for q, sem in enumerate(wq_there):
                sp.dma_start(wq[:, :, quad(q)], dram["L0_xattn_Wq"].rearrange("(k p) n -> p k n", p=P)[:, :, quad(q)]).then_inc(sem, 16)
                if q == 0:
                    sp.dma_start(g2[:, 0:1], dram["L0_xattn_gq"].rearrange("(p a) -> p a", a=1)).then_inc(S.gains, 16)
                    sp.dma_start(g2[:, 1:2], dram["L0_xattn_gk"].rearrange("(p a) -> p a", a=1)).then_inc(S.gains, 16)
                    sp.dma_start(wk[:, :], dram["L0_xattn_Wk"]).then_inc(S.wk, 16)

        @block.gpsimd
        def _(pool):
            nc.gpsimd.memset(T.ident[:, :], 0.0).then_inc(S.consts, 1)
            pool.wait_ge(S.consts, 1)
            nc.gpsimd.affine_select(out=T.ident[:, :], in_=T.ident[:, :], compare_op=ALU.not_equal, fill=1.0,
                                    base=0, pattern=[[-1, P]], channel_multiplier=1).then_inc(S.consts, 1)
            nc.gpsimd.memset(T.ones[:, :], 1.0).then_inc(S.consts, 1)
            nc.gpsimd.memset(T.zero[:, :], 0.0).then_inc(S.consts, 1)
            nc.gpsimd.memset(eps[:, :], EPS).then_inc(S.consts, 1)
            for q in range(KC):
                pool.wait_ge(S.wqh, q + 1)
                nc.gpsimd.tensor_tensor(wql[:, :, quad(q)], wq[:, :, quad(q)], wqh[:, :, quad(q)].bitcast(F32), ALU.subtract).then_inc(S.wql, 1)
                if q == 0:
                    pool.wait_ge(S.gprod, 1)
                    nc.gpsimd.partition_all_reduce(gmax[:, 0:1], T.gcol[:, 0:1], P, ABSMAX).then_inc(S.gmax, 1)
            pool.wait_ge(S.wkh, 1)
            nc.gpsimd.tensor_tensor(T.wkl[:, :], wk[:, :], T.wkh[:, :].bitcast(F32), ALU.subtract).then_inc(S.wkl, 1)

        @block.tensor
        def _(pe):
            pe.wait_ge(S.consts, 3)
            for j in range(NPAIR // PW):
                pe.wait_ge(S.centred, PW * (j + 1))
                bank, slot = turned[j]
                for n in range(PW):
                    for k in range(WC):
                        last = nc.tensor.transpose(bank[:, slot, (k * PW + n) * P:(k * PW + n + 1) * P], xn_of(PW * j + n)[:, k * P:(k + 1) * P], T.ident[:, :])
                    last.then_inc(S.lnT, 1)
            pe.wait_ge(S.wk, 16)
            for q in range(KC):
                if q >= 2:
                    pe.wait_ge(S.wkTl, q - 1)
                for h in range(HB):
                    last = nc.tensor.transpose(psO[:, q % 2, h * P:(h + 1) * P],
                                               wk[:, (HB * q + h) * P:(HB * q + h + 1) * P], T.ident[:, :])
                last.then_inc(S.wkT, 1)
            pe.wait_ge(S.lnTl, NPAIR // PW)
            pe.wait_ge(S.wkTl, KC)

            def step(n, m, o):
                if n is not None:
                    h, g = items[n]
                    if h % HB == 0 and g == 0:
                        pe.wait_ge(S.wql, h // HB + 1)
                    if n >= 2:
                        pe.wait_ge(S.qgl, n - 1)
                    i = 0
                    for k in range(WC):
                        for w, x in ((wqh, xTh), (wql, xTh), (wqh, xTl)):
                            last = nc.tensor.matmul(psK[:, n % 2, :], w[:, k, h * P:(h + 1) * P], x[:, k, g * BANK:(g + 1) * BANK],
                                                    start=(i == 0), stop=(i == 3 * WC - 1))
                            i += 1
                    last.then_inc(S.q, 1)
                if m is not None:
                    pe.wait_ge(S.square, m + 1)
                    if m >= 2:
                        pe.wait_ge(S.newton, m - 1)
                    nc.tensor.matmul(psS[:, m % 2, :], T.ones[:, :], square[:, m % 2, :], start=True, stop=True).then_inc(S.total, 1)
                if o is not None:
                    pe.wait_ge(S.qgl, o + 1)
                    if o >= 2:
                        pe.wait_ge(S.out, o - 1)
                    h = items[o][0]
                    for i, (w, x) in enumerate(((wkTh, qgh), (wkTh, qgl), (wkTl, qgh))):
                        last = nc.tensor.matmul(psO[:, o % 2, :], w[:, h, :], x[:, o % Q_SLOTS, :], start=(i == 0), stop=(i == 2))
                    last.then_inc(S.qw, 1)

            steps(step)

        @block.scalar
        def _(act):
            nc.scalar.preload_act_table_set(LN_EXP)

            def wq_high(q):
                act.wait_ge(wq_there[q], 16)
                nc.scalar.activation(wqh[:, :, quad(q)], wq[:, :, quad(q)], ACT.Copy).then_inc(S.wqh, 1)

            inverse_root_guess(nc, act, L, 0, lx[:, 1, :], lx[:, 2, :], lx[:, 0, :])
            wq_high(0)
            for j in range(NPAIR // PW):
                bank, slot = turned[j]
                act.wait_ge(S.lnT, PW * (j + 1))
                nc.scalar.activation(xTh[:, :, j * PW * P:(j + 1) * PW * P], bank[:, slot, :].rearrange("p (k n) -> p k n", k=WC), ACT.Copy).then_inc(S.lnTh, 1)
            for q in range(KC):
                act.wait_ge(S.wkT, q + 1)
                nc.scalar.activation(wkTh[:, HB * q:HB * (q + 1), :], psO[:, q % 2, :].rearrange("p (h c) -> p h c", c=CD),
                                     ACT.Copy).then_inc(S.wkTh, 1)
                if q:
                    wq_high(q)
            nc.scalar.activation(T.wkh[:, :], wk[:, :], ACT.Copy).then_inc(S.wkh, 1)
            act.wait_ge(S.consts, 5)
            act.wait_ge(S.made, 1)

            def step(n, m, o):
                if n is not None:
                    act.wait_ge(S.q, n + 1)
                    if n >= 2:
                        act.wait_ge(S.total, n - 1)
                    nc.scalar.activation(square[:, n % 2, :], psK[:, n % 2, :], ACT.Square).then_inc(S.square, 1)
                if o is not None:
                    act.wait_ge(S.log, o + 1)
                    if o >= 2:
                        act.wait_ge(S.root, o - 1)
                    nc.scalar.activation(y[:, o % 2, :], log[:, :], ACT.Exp, scale=-0.5).then_inc(S.y, 1)
                if n is not None:
                    if n >= Q_SLOTS:
                        act.wait_ge(S.qw, n - Q_SLOTS + 1)
                    nc.scalar.activation(qgh[:, n % Q_SLOTS, :], psK[:, n % 2, :], ACT.Copy, scale=T.gcol[:, 1:2]).then_inc(S.qgh, 1)
                if o is not None:
                    act.wait_ge(S.y, o + 1)
                    if o:
                        act.wait_ge(S.newton, o)
                    nc.scalar.activation(half[:, :], y[:, o % 2, :], ACT.Square, scale=float(np.sqrt(0.5 / D))).then_inc(S.half, 1)
                if m is not None:
                    act.wait_ge(S.total, m + 1)
                    nc.scalar.activation(log[:, :], psS[:, m % 2, :], ACT.Ln, scale=1.0 / D, bias=eps[:, :]).then_inc(S.log, 1)

            steps(step)

        @block.vector
        def _(dve):
            dve.wait_ge(S.x, 16)
            for i in range(NPAIR):
                nc.vector.bn_stats(stats[:, i, :], T.xs[:, i, :]).then_inc(S.stats, 1)
            for i in range(NPAIR):
                dve.wait_ge(S.stats, i + 1)
                nc.vector.bn_aggr(mv[:, i, :], stats[:, i, :]).then_inc(S.moments, 1)
            dve.wait_ge(S.moments, NPAIR)
            inverse_root_start(nc, dve, L.x, lx[:, 0, :], mv[:, :, 1:2].rearrange("p n a -> p (n a)"), 1)
            inverse_root_end(nc, dve, L, 0, lx[:, 2, :], lx[:, 3, :], lx[:, 0, :], lx[:, 4, :])
            dve.wait_ge(L.root, at(0, 1, 1))
            for i in range(NPAIR):
                if i >= 2:
                    dve.wait_ge(S.lnT, i - 1)
                nc.vector.tensor_scalar(xn_of(i), T.xs[:, i, :], mv[:, i, 0:1], lx[:, 4, i:i + 1],
                                        ALU.subtract, ALU.mult).then_inc(S.centred, 1)
            for j in range(NPAIR // PW):
                bank, slot = turned[j]
                cols = slice(j * PW * P, (j + 1) * PW * P)
                dve.wait_ge(S.lnTh, j + 1)
                nc.vector.tensor_tensor(xTl[:, :, cols], bank[:, slot, :].rearrange("p (k n) -> p k n", k=WC),
                                        xTh[:, :, cols].bitcast(F32), ALU.subtract).then_inc(S.lnTl, 1)
            for q in range(KC):
                dve.wait_ge(S.wkTh, q + 1)
                nc.vector.tensor_tensor(wkTl[:, HB * q:HB * (q + 1), :], psO[:, q % 2, :].rearrange("p (h c) -> p h c", c=CD),
                                        wkTh[:, HB * q:HB * (q + 1), :].bitcast(F32), ALU.subtract).then_inc(S.wkTl, 1)
            dve.wait_ge(S.gains, 32)
            nc.vector.tensor_tensor(T.gcol[:, 0:1], g2[:, 0:1], g2[:, 1:2], ALU.mult).then_inc(S.gprod, 1)
            dve.wait_ge(S.gprod, 1)
            nc.vector.tensor_scalar(T.gcol[:, 1:2], T.gcol[:, 0:1], float(SCALE), None, ALU.mult).then_inc(S.made, 1)
            dve.wait_ge(S.made, 1)
            nc.vector.tensor_copy(T.identb[:, :], T.ident[:, :]).then_inc(S.made, 1)

            def step(n, m, o):
                if o is not None:
                    dve.wait_ge(S.half, o + 1)
                    if o:
                        dve.wait_ge(S.root, o)
                    nc.vector.scalar_tensor_tensor(scaled[:, :], psS[:, o % 2, :], float(D * EPS), half[:, :], ALU.add, ALU.mult).then_inc(S.newton, 1)
                if n is not None:
                    dve.wait_ge(S.qgh, n + 1)
                    nc.vector.scalar_tensor_tensor(qgl[:, n % Q_SLOTS, :], psK[:, n % 2, :], T.gcol[:, 1:2], qgh[:, n % Q_SLOTS, :].bitcast(F32),
                                                   ALU.mult, ALU.subtract).then_inc(S.qgl, 1)
                if o is not None:
                    dve.wait_ge(S.newton, o + 1)
                    nc.vector.scalar_tensor_tensor(root[:, :], scaled[:, :], 1.5, y[:, o % 2, :], ALU.subtract, ALU.mult).then_inc(S.root, 1)
                    dve.wait_ge(S.root, o + 1)
                    dve.wait_ge(S.qw, o + 1)
                    nc.vector.scalar_tensor_tensor(out(o), psO[:, o % 2, :].rearrange("p (m q) -> p m q", q=SQ), -1.0,
                                                   root[:, :].rearrange("p (m q) -> p m q", q=SQ), ALU.mult, ALU.mult).then_inc(S.out, 1)

            steps(step)
            dve.wait_ge(S.gmax, 1)
            nc.vector.tensor_scalar(gmax[:, 1:2], gmax[:, 0:1], -float(np.sqrt(D)), LIMIT, ALU.mult, ALU.add).then_inc(S.made, 1)
            dve.wait_ge(S.made, 3)
            nc.vector.tensor_scalar(T.shift[:, :], gmax[:, 1:2], 0.0, None, ALU.min).then_inc(S.made, 1)



MAIN_SEMS = "ct cth ctl kmm ksq ksum smm zz expd phi pl acc vmm nath nat qh ql oev_a oev_d den dlog dinv dneg dfull norm"


def cross_attention(nc, T, psum, dram):
    psT, psK, psS, psO, psM = psum
    with ExitStack() as ctx:
        def sb(name, shape, dt=F32):
            return ctx.enter_context(nc.sbuf_tensor(f"c_{name}", shape, dt))

        raw = sb("raw", [ROWS, 2, NT, CD])
        ch, cl = sb("ch", [ROWS, 2, NT, CD], F32R), sb("cl", [ROWS, 2, NT, CD], F32R)
        cTh, cTl = sb("cTh", [CD, CT_SLOTS, ROWS], F32R), sb("cTl", [CD, CT_SLOTS, ROWS], F32R)
        qwh, qwl = sb("qwh", [CD, 2, HQ], F32R), sb("qwl", [CD, 2, HQ], F32R)
        sq = sb("sq", [ROWS, 2, INNER])
        ss = sb("ss", [ROWS, 2, 6, H])
        prob = sb("prob", [ROWS, 2, HQ])
        ph, pl = sb("ph", [ROWS, 2, HQ], F32R), sb("pl", [ROWS, 2, HQ], F32R)
        acc = sb("acc", [ROWS, 2, HQ])
        den = sb("den", [P, 4, BANK])
        W, S, R = primed(nc, ctx, ("wc", "zeroed loaded00 loaded01 loaded10 loaded11 passed"), ("main", MAIN_SEMS), ("keyrms", ROOT))
        loaded = ((W.loaded00, W.loaded01), (W.loaded10, W.loaded11))
        block = ctx.enter_context(nc.Block())
        ctx_rows = dram["ctx_1024"]

        def done(i, t, per, k=None):
            return at(i, per * TP, per * t + (per if k is None else k))

        def batch_done(i, batch, per=1, k=None):
            return at(i, 2 * per, per * batch + (per if k is None else k))

        def more(i, batch):
            return batch < 2 or not isinstance(i, int) or i < NPAIR - 1

        def steps(i, last):
            for t in range(LAG, TP if last else TP + LAG):
                yield tuple(u if not last or u < TP else None for u in (t, t + 2, t + 3, t + 4, t + 5))

        def pipeline(eng, emit, end=None, begin=None):
            for t in range(-5, LAG):
                emit(0, *(u if u >= 0 else None for u in (t, t + 2, t + 3, t + 4, t + 5)))
                if begin is not None and t < 0:
                    begin(t + 5)
            with eng.Fori(0, NPAIR - 1) as i:
                for v in steps(i, False):
                    emit(i, *v)
            for v in steps(NPAIR - 1, True):
                emit(NPAIR - 1, *v)
            if end is not None:
                for half in range(2):
                    end(NPAIR - 1, 1, half)

        def out_half(i, batch, half):
            pair, b = i + batch // 2, batch % 2
            big = T.big[:, :].rearrange("p (n b m) -> p n b m", b=2, m=HQ)
            n = slice(pair, pair + 1) if isinstance(pair, int) else bass.ds(pair, 1)
            return big[:, n, b, half * BANK:(half + 1) * BANK].rearrange("p n m -> p (n m)")

        @block.sync
        def _(sp):
            sp.wait_ge(W.zeroed, 1)

            def load(i, b):
                one = ctx_rows[bass.ds(2 * i + b, 1)] if not isinstance(i, int) else ctx_rows[2 * i + b:2 * i + b + 1]
                sp.dma_start(raw[0:FULL, b, :, :], one[:, 0:FULL * NT, :].rearrange("n (p t) c -> p (n t) c", t=NT))\
                  .then_inc(loaded[b][0], 16)
                sp.dma_start(raw[FULL:ROWS, b, 0:REST, :], one[:, FULL * NT:SKV, :]).then_inc(loaded[b][1], 16)

            for b in range(2):
                load(0, b)
            with sp.Fori(0, NPAIR - 1) as i:
                for b in range(2):
                    sp.wait_ge(S.ct, done(i, NT * (b + 1) - 1, 1))
                    alone(sp, W.passed)
                    sp.wait_ge(S.nat, batch_done(i, b, len(PIECES)))
                    load(i + 1, b)

        @block.tensor
        def _(pe):
            def key_chunk(i, k, c):
                slot = CT_SLOT[k % TP]
                if c == 0:
                    pe.wait_ge(S.ctl, done(i, k, 1))
                pe.wait_ge(S.ksq, done(i, k, KC, c - 1))
                cols = slice(c * BANK, (c + 1) * BANK)
                for n, (x, w) in enumerate(((cTh, T.wkh), (cTh, T.wkl), (cTl, T.wkh))):
                    last = nc.tensor.matmul(psK[0:ROWS, c % 2, :], x[:, slot, :], w[:, cols], start=(n == 0), stop=(n == 2))
                last.then_inc(S.kmm, 1)

            def score_half(i, s, half):
                slot, b = CT_SLOT[s % TP], s % TP // NT
                if s % NT == 0 and half == 0:
                    pe.wait_ge(S.qh, batch_done(i, s // NT, 2))
                    pe.wait_ge(S.ql, batch_done(i, s // NT, 2))
                pe.wait_ge(S.zz, done(i, s, 2, half - 1))
                cols = slice(half * BANK, (half + 1) * BANK)
                for n, (x, w) in enumerate(((cTh, qwh), (cTh, qwl), (cTl, qwh))):
                    last = nc.tensor.matmul(psS[0:ROWS, half, :], x[:, slot, :], w[:, b, cols], start=(n == 0), stop=(n == 2))
                last.then_inc(S.smm, 1)

            def weigh_half(i, v, half):
                batch, b, tile, rows = v // NT, v % TP // NT, v % NT, rows_of(v)
                if half == 0:
                    pe.wait_ge(S.pl, done(i, v, 1))
                    if tile == 0:
                        pe.wait_ge(S.nat, batch_done(i, batch, len(PIECES)))
                        pe.wait_ge(S.oev_a, batch_done(i, batch - 1))
                        pe.wait_ge(S.oev_d, batch_done(i, batch - 1))
                cols = slice(half * BANK, (half + 1) * BANK)
                for n, (x, w) in enumerate(((ch, ph), (ch, pl), (cl, ph))):
                    last = nc.tensor.matmul(psO[:, half, :], x[0:rows, b, tile, :], w[0:rows, v % 2, cols],
                                            start=(tile == 0 and n == 0), stop=(tile == NT - 1 and n == 2))
                if half:
                    last.then_inc(S.vmm, 1)

            def denominators(i, batch, half):
                if half == 0:
                    pe.wait_ge(S.acc, done(i, NT * (batch + 1) - 1, 1))
                pe.wait_ge(S.dneg, batch_done(i, batch, 2, half))
                nc.tensor.matmul(psM[:, :], T.ones[0:ROWS, :], acc[:, batch % 2, half * BANK:(half + 1) * BANK],
                                 start=True, stop=True).then_inc(S.den, 1)

            def step(i, v, s, r, k, x):
                if x is not None:
                    if x % NT == 0:
                        pair, b = x // TP, x % TP // NT
                        for k2 in range(2):
                            pe.wait_ge(loaded[b][k2], 16 * i + 16 * (pair + 1))
                    pe.wait_ge(S.ctl, done(i, x - 1, 1))
                    nc.tensor.transpose(psT[:, 0:ROWS], raw[:, x % TP // NT, x % NT, :],
                                        T.ident[0:ROWS, 0:ROWS]).then_inc(S.ct, 1)
                if k is not None:
                    key_chunk(i, k, 0)
                if s is not None:
                    score_half(i, s, 0)
                if k is not None:
                    key_chunk(i, k, 1)
                if s is not None:
                    score_half(i, s, 1)
                if k is not None:
                    key_chunk(i, k, 2)
                if v is not None:
                    weigh_half(i, v, 0)
                if k is not None:
                    key_chunk(i, k, 3)
                if v is not None:
                    weigh_half(i, v, 1)
                if v is not None:
                    if v % NT == NT - 1:
                        denominators(i, v // NT, 0)
                    elif v % NT == 3 and v > NT:
                        denominators(i, v // NT - 1, 1)

            def end(i, batch, half):
                if half:
                    denominators(i, batch, half)

            pipeline(pe, step, end)

        @block.scalar
        def _(act):
            nc.scalar.preload_act_table_set(LN_EXP)

            def square(i, k, c):
                act.wait_ge(S.kmm, done(i, k, KC, c + 1))
                act.wait_ge(S.ksum, done(i, k - 2, 2, c // 2 + 1))
                nc.scalar.activation(sq[:, k % 2, c * BANK:(c + 1) * BANK], psK[0:ROWS, c % 2, :], ACT.Square).then_inc(S.ksq, 1)

            def exponentials(i, s):
                act.wait_ge(S.zz, done(i, s, 2))
                nc.scalar.activation(prob[:, s % 2, :], prob[:, s % 2, :], ACT.Exp, bias=T.shift[0:ROWS, :]).then_inc(S.expd, 1)

            def probs_high(i, s):
                act.wait_ge(S.expd, done(i, s, 1))
                act.wait_ge(S.vmm, done(i, s - 2, 1))
                nc.scalar.activation(ph[:, s % 2, :], prob[:, s % 2, :], ACT.Copy).then_inc(S.phi, 1)

            def query_high(i, batch, half):
                b = batch % 2
                heads = slice(half * H // 2, (half + 1) * H // 2)
                act.wait_ge(S.smm, done(i, NT * (batch - 1) - 1, 2))
                pair = i + batch // 2
                src = T.queries[:, bass.ds(pair, 1), b, heads, :] if not isinstance(pair, int) else T.queries[:, pair:pair + 1, b, heads, :]
                nc.scalar.activation(qwh[:, b, half * BANK:(half + 1) * BANK], src.rearrange("p n h q -> p (n h q)"), ACT.Copy).then_inc(S.qh, 1)

            def context_high(i, batch, piece):
                b = batch % 2
                if piece == 0:
                    for k2 in range(2):
                        act.wait_ge(loaded[b][k2], 16 * i + 16 * (batch // 2 + 1))
                    act.wait_ge(S.vmm, done(i, NT * (batch - 1) - 1, 1))
                nc.scalar.activation(ch[:, b, PIECES[piece], :], raw[:, b, PIECES[piece], :], ACT.Copy).then_inc(S.nath, 1)

            def step(i, v, s, r, k, x):
                e = s - 1 if s is not None and s > 0 else TP - 1 if s is None and v == TP - 2 else None
                if e is not None:
                    exponentials(i, e)
                if k is not None:
                    square(i, k, 0)
                if e is not None:
                    probs_high(i, e)
                if k is not None:
                    square(i, k, 1)
                if x is not None:
                    act.wait_ge(S.ct, done(i, x, 1))
                    act.wait_ge(S.smm, done(i, x - ct_before(x), 2))
                    nc.scalar.activation(cTh[:, CT_SLOT[x % TP], :], psT[:, 0:ROWS], ACT.Copy).then_inc(S.cth, 1)
                if r is not None:
                    n = at(i, TP, r) - CREDIT
                    inverse_root_guess(nc, act, R, n, ss[:, r % 2, 2, :], ss[:, r % 2, 3, :], ss[:, r % 2, 1, :])
                if k is not None:
                    square(i, k, 2)
                    square(i, k, 3)
                if v is not None and v % NT == NT - 1:
                    evacuate(i, v // NT)
                if v is not None:
                    batch, n = v // NT, v % NT
                    if batch and n in (0, 4):
                        logarithms(i, batch - 1, n // 4)
                    if batch and n in (1, 5):
                        inverses(i, batch - 1, n // 4)
                    if n in (6, 7) and more(i, batch + 1):
                        query_high(i, batch + 1, n - 6)
                    if n in CONTEXT_HIGH and more(i, batch + 1):
                        context_high(i, batch + 1, CONTEXT_HIGH.index(n))

            def end(i, batch, half):
                logarithms(i, batch, half)
                inverses(i, batch, half)

            def logarithms(i, batch, half):
                act.wait_ge(S.den, batch_done(i, batch, 2, half + 1))
                nc.scalar.activation(den[:, 0, :], psM[:, :], ACT.Ln).then_inc(S.dlog, 1)

            def inverses(i, batch, half):
                act.wait_ge(S.dlog, batch_done(i, batch, 2, half + 1))
                act.wait_ge(S.dfull, batch_done(i, batch, 2, half))
                nc.scalar.activation(den[:, 1, :], den[:, 0, :], ACT.Exp, scale=-1.0).then_inc(S.dinv, 1)

            def evacuate(i, batch):
                act.wait_ge(S.vmm, done(i, NT * (batch + 1) - 1, 1))
                act.wait_ge(S.ql, batch_done(i, batch, 2))
                alone(act, W.passed)
                dst = out_half(i, batch, 0)
                nc.scalar.activation(dst, psO[:, 0, :], ACT.Copy).then_inc(S.oev_a, 1)

            def begin(n):
                if n in (0, 1):
                    query_high(0, 0, n)
                if n:
                    context_high(0, 0, n - 1)

            pipeline(act, step, end, begin)

        @block.vector
        def _(dve):
            nc.vector.memset(raw[:, :, :, :], 0.0).then_inc(W.zeroed, 1)

            def context_low(i, batch, piece):
                b = batch % 2
                dve.wait_ge(S.nath, batch_done(i, batch, len(PIECES), piece + 1))
                nc.vector.tensor_tensor(cl[:, b, PIECES[piece], :], raw[:, b, PIECES[piece], :],
                                        ch[:, b, PIECES[piece], :].bitcast(F32), ALU.subtract).then_inc(S.nat, 1)

            def query_low(i, batch, half):
                b = batch % 2
                heads, cols = slice(half * H // 2, (half + 1) * H // 2), slice(half * BANK, (half + 1) * BANK)
                dve.wait_ge(S.qh, batch_done(i, batch, 2, half + 1))
                dve.wait_ge(S.smm, done(i, NT * (batch - 1) - 1, 2))
                pair = i + batch // 2
                src = T.queries[:, bass.ds(pair, 1), b, heads, :] if not isinstance(pair, int) else T.queries[:, pair:pair + 1, b, heads, :]
                nc.vector.tensor_tensor(qwl[:, b, cols], src.rearrange("p n h q -> p (n h q)"), qwh[:, b, cols].bitcast(F32),
                                        ALU.subtract).then_inc(S.ql, 1)

            def key_sums(i, k, part):
                dve.wait_ge(S.ksq, done(i, k, KC, 2 * part + 2))
                dve.wait_ge(R.x, done(i, k - 2, 1))
                nc.vector.tensor_reduce(ss[:, k % 2, 0, 8 * part:8 * part + 8],
                                        sq[:, k % 2, part * 2 * BANK:(part + 1) * 2 * BANK].rearrange("p (h d) -> p h d", d=D),
                                        AX.X, ALU.add).then_inc(S.ksum, 1)

            def scale_scores(i, s, half):
                cols = slice(half * BANK, (half + 1) * BANK)
                if half == 0:
                    dve.wait_ge(R.root, done(i, s, 1))
                    dve.wait_ge(S.acc, done(i, s - 2, 1))
                dve.wait_ge(S.smm, done(i, s, 2, half + 1))
                nc.vector.tensor_tensor(prob[:, s % 2, cols].rearrange("p (h q) -> p h q", q=SQ),
                                        psS[0:ROWS, half, :].rearrange("p (h q) -> p h q", q=SQ),
                                        over(ss[:, s % 2, 5, 8 * half:8 * half + 8], SQ), ALU.mult).then_inc(S.zz, 1)

            def evacuate(i, batch):
                dve.wait_ge(S.vmm, done(i, NT * (batch + 1) - 1, 1))
                alone(dve, W.passed)
                nc.vector.tensor_copy(out_half(i, batch, 1), psO[:, 1, :]).then_inc(S.oev_d, 1)

            def step(i, v, s, r, k, x):
                if r is not None:
                    key_sums(i, r, 1)
                    dve.wait_ge(S.ksum, done(i, r, 2))
                    inverse_root_start(nc, dve, R.x, ss[:, r % 2, 1, :], ss[:, r % 2, 0, :], D)
                if s is not None:
                    scale_scores(i, s, 0)
                if k is not None:
                    key_sums(i, k, 0)
                if x is not None:
                    dve.wait_ge(S.cth, done(i, x, 1))
                    dve.wait_ge(S.smm, done(i, x - ct_before(x), 2))
                    nc.vector.tensor_tensor(cTl[:, CT_SLOT[x % TP], :], psT[:, 0:ROWS], cTh[:, CT_SLOT[x % TP], :].bitcast(F32),
                                            ALU.subtract).then_inc(S.ctl, 1)
                if s is not None:
                    scale_scores(i, s, 1)
                if r is not None:
                    n = at(i, TP, r) - CREDIT
                    inverse_root_end(nc, dve, R, n, ss[:, r % 2, 3, :], ss[:, r % 2, 4, :], ss[:, r % 2, 1, :], ss[:, r % 2, 5, :])
                if v is not None and v % NT == NT - 1:
                    evacuate(i, v // NT)
                if v is not None:
                    batch, n = v // NT, v % NT
                    if batch and n in (2, 6):
                        newton_start(i, batch - 1, n // 4)
                    if batch and n in (3, 7):
                        newton_end(i, batch - 1, n // 4)
                    if n in (8, 9) and more(i, batch + 1):
                        query_low(i, batch + 1, n - 8)
                    if n in CONTEXT_LOW and more(i, batch + 1):
                        context_low(i, batch + 1, CONTEXT_LOW.index(n))

            def end(i, batch, half):
                newton_start(i, batch, half)
                newton_end(i, batch, half)

            def newton_start(i, batch, half):
                dve.wait_ge(S.dinv, batch_done(i, batch, 2, half + 1))
                nc.vector.scalar_tensor_tensor(den[:, 2, :], psM[:, :], -1.0, den[:, 1, :], ALU.mult, ALU.mult).then_inc(S.dneg, 1)

            def newton_end(i, batch, half):
                dve.wait_ge(S.dneg, batch_done(i, batch, 2, half + 1))
                dve.wait_ge(S.norm, batch_done(i, batch, 2, half))
                nc.vector.scalar_tensor_tensor(den[:, 3, :], den[:, 2, :], 2.0, den[:, 1, :], ALU.add, ALU.mult).then_inc(S.dfull, 1)

            def begin(n):
                if n in (0, 1):
                    query_low(0, 0, n)
                if n:
                    context_low(0, 0, n - 1)

            pipeline(dve, step, end, begin)

        @block.gpsimd
        def _(pool):
            def step(i, v, s, r, k, x):
                if s is not None and s > 0:
                    low_and_sum(i, s - 1)
                elif s is None and v == TP - 2:
                    low_and_sum(i, TP - 1)
                if v is not None and v % NT in (4, 8) and v >= NT:
                    normalise(i, v // NT - 1, v % NT // 8)

            def normalise(i, batch, half):
                pool.wait_ge(S.dfull, batch_done(i, batch, 2, half + 1))
                pool.wait_ge((S.oev_a, S.oev_d)[half], batch_done(i, batch))
                out = out_half(i, batch, half)
                nc.gpsimd.tensor_tensor(out, out, den[:, 3, :], ALU.mult).then_inc(S.norm, 1)

            def low_and_sum(i, s):
                batch, rows = s // NT, rows_of(s)
                pool.wait_ge(S.phi, done(i, s, 1))
                pool.wait_ge(S.vmm, done(i, s - 2, 1))
                nc.gpsimd.tensor_tensor(pl[:, s % 2, :], prob[:, s % 2, :], ph[:, s % 2, :].bitcast(F32), ALU.subtract).then_inc(S.pl, 1)
                if s % NT == 0:
                    pool.wait_ge(S.den, batch_done(i, batch - 2, 2))
                    nc.gpsimd.tensor_tensor(acc[:, batch % 2, :], prob[:, s % 2, :], T.zero[0:ROWS, :].broadcast_to([ROWS, HQ]), ALU.add).then_inc(S.acc, 1)
                else:
                    pool.wait_ge(S.acc, done(i, s - 1, 1))
                    nc.gpsimd.tensor_tensor(acc[0:rows, batch % 2, :], acc[0:rows, batch % 2, :], prob[0:rows, s % 2, :], ALU.add).then_inc(S.acc, 1)

            pipeline(pool, step, normalise)



HEAD_SEMS = ("w0 w1 w2 w3 wqkv vT vTh vTl woh wol wvo wvoh wvol oh ol out outT back x2 high low passed")
OUT_SEMS = "stats moments centred lnT lnTh lnTl qkvmm qkv_a qkv_b amax"
QUADS = H // HB
O_SLOTS = 4


def project(nc, T, psum, dram):
    psT, psK, psS, psO, psM = psum
    with ExitStack() as ctx:
        def sb(name, shape, dt=F32):
            return ctx.enter_context(nc.sbuf_tensor(f"o_{name}", shape, dt))

        vTh, vTl = sb("vTh", [P, 2, HB, P], F32R), sb("vTl", [P, 2, HB, P], F32R)
        woh, wol = sb("woh", [P, 2, HB, DIM], F32R), sb("wol", [P, 2, HB, DIM], F32R)
        wvoh, wvol = sb("wvoh", [P, 2, HB, DIM], F32R), sb("wvol", [P, 2, HB, DIM], F32R)
        oh, ol = sb("oh", [P, O_SLOTS, BANK], F32R), sb("ol", [P, O_SLOTS, BANK], F32R)
        outT = sb("outT", [P, WC, NPAIR * P])
        wqkv = sb("wqkv", [P, WC, 3 * DIM])
        wqkvh, wqkvl = sb("wqkvh", [P, WC, 3 * DIM], F32R), sb("wqkvl", [P, WC, 3 * DIM], F32R)
        stats, mv, lx = sb("stats", [P, 6]), sb("mv", [P, 2]), sb("lx", [P, 5, 1])
        xn = sb("xn", [P, WC, P])
        xTh, xTl = sb("xTh", [P, WC, P], F32R), sb("xTl", [P, WC, P], F32R)
        W, S, L = primed(nc, ctx, ("heads", HEAD_SEMS), ("out", OUT_SEMS), ("outln", ROOT))
        flat = T.qkv[:, :, :].rearrange("p n m -> p (n m)")
        wv = flat[:, 0:INNER].rearrange("p (h d) -> p h d", d=D)
        wo = flat[:, INNER:INNER + H * DIM].rearrange("p (h n) -> p h n", n=DIM)
        loaded = (W.w0, W.w1, W.w2, W.w3)
        items = [(h, g) for h in range(H) for g in range(GROUPS)]
        per_quad = HB * GROUPS
        sums = (psK, psS)
        block = ctx.enter_context(nc.Block())

        def heads(q):
            return slice(HB * q, HB * (q + 1))

        def weighed(h, g):
            return T.queries[:, g * GP:(g + 1) * GP, :, h, :].rearrange("p n b q -> p (n b) q")

        def item(x, n):
            return x[:, n % O_SLOTS, :].rearrange("p (m q) -> p m q", q=SQ)

        def flatten(x):
            return x.rearrange("p h n -> p (h n)")

        def pipeline(matrices, products):
            for q in range(QUADS + 1):
                if q < QUADS:
                    matrices(q)
                if q:
                    products(q - 1)

        def normed(eng, step):
            step(0, None)
            with eng.Fori(0, NPAIR - 1) as i:
                step(i + 1, i)
            step(None, NPAIR - 1)

        @block.sync
        def _(sp):
            for q in range(QUADS):
                sp.dma_start(wv[:, heads(q), :], dram["L0_xattn_Wv"].rearrange("p (h d) -> p h d", d=D)[:, heads(q), :]).then_inc(loaded[q], 16)
                sp.dma_start(wo[:, heads(q), :], dram["L0_xattn_Wo"].rearrange("(h p) n -> p h n", p=P)[:, heads(q), :]).then_inc(loaded[q], 16)
            sp.dma_start(wqkv[:, :, :], dram["L0_attn_W_qkv"].rearrange("(k p) n -> p k n", p=P)).then_inc(W.wqkv, 16)

        @block.tensor
        def _(pe):
            def matrices(q):
                pe.wait_ge(loaded[q], 32)
                if q:
                    pe.wait_ge(W.vTl, q)
                for h in range(HB):
                    last = nc.tensor.transpose(psT[:, h * P:(h + 1) * P], wv[:, HB * q + h, :], T.ident[:, :])
                last.then_inc(W.vT, 1)
                pe.wait_ge(W.vTl, q + 1)
                pe.wait_ge(W.wol, q + 1)
                for j in range(HB // PW):
                    if q:
                        pe.wait_ge(W.wvol, (HB // PW) * (q - 1) + j + 1)
                    for m in range(PW):
                        h = PW * j + m
                        for n, (x, w) in enumerate(((vTh, woh), (vTh, wol), (vTl, woh))):
                            last = nc.tensor.matmul(psO[:, j, m * DIM:(m + 1) * DIM], x[:, q % 2, h, :], w[:, q % 2, h, :],
                                                    start=(n == 0), stop=(n == 2))
                    last.then_inc(W.wvo, 1)

            def products(q):
                pe.wait_ge(W.wvol, (HB // PW) * (q + 1))
                for n in range(per_quad * q, per_quad * (q + 1)):
                    h, g = items[n]
                    pe.wait_ge(W.ol, n + 1)
                    for c in range(WC):
                        cols = slice(c * P, (c + 1) * P)
                        for m, (w, x) in enumerate(((wvoh, oh), (wvol, oh), (wvoh, ol))):
                            last = nc.tensor.matmul(sums[g][:, c, :], w[:, q % 2, h % HB, cols], x[:, n % O_SLOTS, :],
                                                    start=(h == 0 and m == 0), stop=(h == H - 1 and m == 2))
                    last.then_inc(W.out, 1)

            pipeline(matrices, products)
            pe.wait_ge(W.outT, WC * GROUPS)
            for j in range(NPAIR // PW):
                bank = (psT, psM)[j % 2]
                if j >= 2:
                    pe.wait_ge(W.x2, j - 1)
                for n in range(PW):
                    for k in range(WC):
                        pair = PW * j + n
                        last = nc.tensor.transpose(bank[:, (n * WC + k) * P:(n * WC + k + 1) * P], outT[:, k, pair * P:(pair + 1) * P], T.ident[:, :])
                last.then_inc(W.back, 1)
            pe.wait_ge(W.low, 1)

            def step(a, b):
                if b is None:
                    return
                pe.wait_ge(S.centred, at(b, 1, 1))
                pe.wait_ge(S.lnTl, at(b, 1, 0))
                for k in range(WC):
                    last = nc.tensor.transpose(psT[:, k * P:(k + 1) * P], xn[:, k, :], T.ident[:, :])
                last.then_inc(S.lnT, 1)
                pe.wait_ge(S.lnTl, at(b, 1, 1))
                for j, (cols, out) in enumerate(((slice(0, 2 * DIM), psO[:, 0, :]), (slice(2 * DIM, 3 * DIM), psO[:, 1, 0:DIM]))):
                    pe.wait_ge(S.amax, at(b, 2, j - 1))
                    n = 0
                    for k in range(WC):
                        for x, w in ((xTh, wqkvh), (xTh, wqkvl), (xTl, wqkvh)):
                            last = nc.tensor.matmul(out, x[:, k, :], w[:, k, cols], start=(n == 0), stop=(n == 3 * WC - 1))
                            n += 1
                    last.then_inc(S.qkvmm, 1)

            normed(pe, step)

        @block.scalar
        def _(act):
            nc.scalar.preload_act_table_set(LN_EXP)

            def weighed_high(n):
                if n >= O_SLOTS:
                    act.wait_ge(W.out, n - O_SLOTS + 1)
                nc.scalar.activation(item(oh, n), weighed(*items[n]), ACT.Copy).then_inc(W.oh, 1)

            def matrices(q):
                act.wait_ge(loaded[q], 32)
                if q >= 2:
                    act.wait_ge(W.wvo, (HB // PW) * (q - 1))
                nc.scalar.activation(flatten(woh[:, q % 2, :, :]), flatten(wo[:, heads(q), :]), ACT.Copy).then_inc(W.woh, 1)
                act.wait_ge(W.vT, q + 1)
                nc.scalar.activation(flatten(vTh[:, q % 2, :, :]), psT[:, :], ACT.Copy).then_inc(W.vTh, 1)
                for j in range(HB // PW):
                    act.wait_ge(W.wvo, (HB // PW) * q + j + 1)
                    if q >= 2:
                        act.wait_ge(W.out, per_quad * (q - 1))
                    nc.scalar.activation(flatten(wvoh[:, q % 2, PW * j:PW * (j + 1), :]), psO[:, j, :], ACT.Copy).then_inc(W.wvoh, 1)

            def products(q):
                for n in range(per_quad * q + (O_SLOTS if q else 0), min(per_quad * (q + 1) + O_SLOTS, len(items))):
                    weighed_high(n)

            pipeline(matrices, products)
            for g in range(GROUPS):
                if g == 0:
                    act.wait_ge(W.out, len(items))
                nc.scalar.activation(outT[:, 0, g * BANK:(g + 1) * BANK], sums[g][:, 0, :], ACT.Copy).then_inc(W.outT, 1)
            act.wait_ge(W.wqkv, 16)
            nc.scalar.activation(flatten(wqkvh[:, :, :]), flatten(wqkv[:, :, :]), ACT.Copy).then_inc(W.high, 1)

            def step(a, b):
                if b is not None:
                    n = slice(b, b + 1) if isinstance(b, int) else bass.ds(b, 1)
                    act.wait_ge(S.lnT, at(b, 1, 1))
                    nc.scalar.activation(xTh[:, :, :], psT[:, 0:WC * P].rearrange("p (k n) -> p k n", k=WC), ACT.Copy).then_inc(S.lnTh, 1)
                if a is not None:
                    inverse_root_guess(nc, act, L, a, lx[:, 1, :], lx[:, 2, :], lx[:, 0, :])
                if b is not None:
                    act.wait_ge(S.qkvmm, at(b, 2, 1))
                    nc.scalar.activation(T.qkv[:, n, 0:2 * DIM].rearrange("p n m -> p (n m)"), psO[:, 0, :], ACT.Copy).then_inc(S.qkv_a, 1)
                    act.wait_ge(S.qkvmm, at(b, 2, 2))
                    nc.scalar.activation(T.qkv[:, n, 2 * DIM:3 * DIM].rearrange("p n m -> p (n m)"), psO[:, 1, 0:DIM], ACT.Copy).then_inc(S.qkv_b, 1)

            act.wait_ge(W.wvo, (HB // PW) * QUADS)
            normed(act, step)

        @block.vector
        def _(dve):
            def weighed_low(n):
                dve.wait_ge(W.oh, n + 1)
                nc.vector.tensor_tensor(item(ol, n), weighed(*items[n]), item(oh, n).bitcast(F32), ALU.subtract).then_inc(W.ol, 1)

            def matrices(q):
                dve.wait_ge(W.woh, q + 1)
                nc.vector.tensor_tensor(flatten(wol[:, q % 2, :, :]), flatten(wo[:, heads(q), :]), flatten(woh[:, q % 2, :, :]).bitcast(F32),
                                        ALU.subtract).then_inc(W.wol, 1)
                dve.wait_ge(W.vTh, q + 1)
                nc.vector.tensor_tensor(flatten(vTl[:, q % 2, :, :]), psT[:, :], flatten(vTh[:, q % 2, :, :]).bitcast(F32),
                                        ALU.subtract).then_inc(W.vTl, 1)
                for j in range(HB // PW):
                    slot = slice(PW * j, PW * (j + 1))
                    dve.wait_ge(W.wvoh, (HB // PW) * q + j + 1)
                    nc.vector.tensor_tensor(flatten(wvol[:, q % 2, slot, :]), psO[:, j, :], flatten(wvoh[:, q % 2, slot, :]).bitcast(F32),
                                            ALU.subtract).then_inc(W.wvol, 1)

            def products(q):
                for n in range(per_quad * q + (O_SLOTS if q else 0), min(per_quad * (q + 1) + O_SLOTS, len(items))):
                    weighed_low(n)

            pipeline(matrices, products)
            for g in range(GROUPS):
                if g == 0:
                    dve.wait_ge(W.out, len(items))
                nc.vector.tensor_copy(outT[:, 1, g * BANK:(g + 1) * BANK], sums[g][:, 1, :]).then_inc(W.outT, 1)
            for j in range(NPAIR // PW):
                x = T.xs[:, PW * j:PW * (j + 1), :].rearrange("p n c -> p (n c)")
                dve.wait_ge(W.back, j + 1)
                nc.vector.tensor_tensor(x, x, (psT, psM)[j % 2][:, :], ALU.add).then_inc(W.x2, 1)
            dve.wait_ge(W.high, 1)
            nc.vector.tensor_tensor(flatten(wqkvl[:, :, :]), flatten(wqkv[:, :, :]), flatten(wqkvh[:, :, :]).bitcast(F32),
                                    ALU.subtract).then_inc(W.low, 1)
            dve.wait_ge(W.x2, NPAIR // PW)

            def step(a, b):
                if b is not None:
                    dve.wait_ge(S.lnTh, at(b, 1, 1))
                    nc.vector.tensor_tensor(xTl[:, :, :], psT[:, 0:WC * P].rearrange("p (k n) -> p k n", k=WC),
                                            xTh[:, :, :].bitcast(F32), ALU.subtract).then_inc(S.lnTl, 1)
                if a is not None:
                    n = slice(a, a + 1) if isinstance(a, int) else bass.ds(a, 1)
                    x = T.xs[:, n, :].rearrange("p n c -> p (n c)")
                    nc.vector.bn_stats(stats[:, :], x).then_inc(S.stats, 1)
                    dve.wait_ge(S.stats, at(a, 1, 1))
                    alone(dve, W.passed)
                    nc.vector.bn_aggr(mv[:, :], stats[:, :]).then_inc(S.moments, 1)
                    dve.wait_ge(S.moments, at(a, 1, 1))
                    inverse_root_start(nc, dve, L.x, lx[:, 0, :], mv[:, 1:2], 1)
                if a is not None:
                    inverse_root_end(nc, dve, L, a, lx[:, 2, :], lx[:, 3, :], lx[:, 0, :], lx[:, 4, :])
                    dve.wait_ge(L.root, at(a, 1, 1))
                    dve.wait_ge(S.lnT, at(a, 1, 0))
                    nc.vector.tensor_scalar(xn[:, :, :].rearrange("p k n -> p (k n)"), x, mv[:, 0:1], lx[:, 4, :],
                                            ALU.subtract, ALU.mult).then_inc(S.centred, 1)
                if b is not None:
                    n = slice(b, b + 1) if isinstance(b, int) else bass.ds(b, 1)
                    amax = T.amax[:, n, :].rearrange("p n g -> p (n g)")
                    dve.wait_ge(S.qkv_a, at(b, 1, 1))
                    nc.vector.tensor_reduce(amax[:, 0:2], psO[:, 0, :].rearrange("p (g n) -> p g n", g=2), AX.X, ALU.max,
                                            apply_absolute_value=True).then_inc(S.amax, 1)
                    dve.wait_ge(S.qkv_b, at(b, 1, 1))
                    nc.vector.tensor_reduce(amax[:, 2:3], psO[:, 1, 0:DIM], AX.X, ALU.max, apply_absolute_value=True).then_inc(S.amax, 1)

            normed(dve, step)



HH = P // DS
NC = HS // HH
VB = 2 * DS + 2
SM_SEMS = "smm smax sub exp inv pT pTe vbd pv"
ATT_SEMS = "u expo magic sum q8 T qT kbd dup o oT oTe proj x3"
FFN_SEMS = ("stats moments centred lnT lnTe mm gmax eq cand first ind gsub gexp gsum gtop q kw ks vw vs vtop krep T "
            "qT kbd dup y")


def scores_pe(nc, pe, S, scores, qT, kbd, start=True):
    for b in range(2):
        for c in range(NC):
            last = nc.tensor.matmul(scores[b * SQ:(b + 1) * SQ, c, :], qT[:, c, b * SQ:(b + 1) * SQ], kbd(c, b),
                                    start=start, stop=True)
    last.then_inc(S.smm, 1)


def transpose_pe(nc, pe, T, S, i, out, prob):
    pe.wait_ge(S.exp, at(i, 1, 1))
    for c in range(NC):
        for m in range(HS // 4):
            last = nc.tensor.transpose(out[:, c, m * P:(m + 1) * P], prob[:, (4 * c + m) * P:(4 * c + m + 1) * P], T.ident[:, :])
        last.then_inc(S.pT, 1)


def weigh_pe(nc, pe, S, i, out, pT, vbd):
    pe.wait_ge(S.vbd, at(i, 1, 1))
    for m in range(HS // 2):
        if m % 4 == 0:
            pe.wait_ge(S.pTe, at(i, NC, m // 4 + 1))
        for b in range(2):
            last = nc.tensor.matmul(out[b * SQ:(b + 1) * SQ, m * VB:(m + 1) * VB],
                                    pT[:, m, b * SQ:(b + 1) * SQ], vbd(b, m), start=True, stop=True)
    last.then_inc(S.pv, 1)


def transposed_act(nc, act, S, i, dst, src):
    for c in range(NC):
        act.wait_ge(S.pT, at(i, NC, c + 1))
        nc.scalar.activation(dst[:, 4 * c:4 * c + 4, :].rearrange("p m n -> p (m n)"), src[:, c, :], ACT.Copy).then_inc(S.pTe, 1)


def softmax_dve(nc, dve, S, i, scores, shifted, st):
    dve.wait_ge(S.smm, at(i, 1, 1))
    nc.vector.tensor_reduce(st[:, 0, :], scores.rearrange("p (h k) -> p h k", k=SQ), AX.X, ALU.max).then_inc(S.smax, 1)
    dve.wait_ge(S.smax, at(i, 1, 1))
    dve.wait_ge(S.pT, at(i, NC, 0))
    nc.vector.tensor_tensor(shifted.rearrange("p (h k) -> p h k", k=SQ), scores.rearrange("p (h k) -> p h k", k=SQ),
                            over(st[:, 0, :], SQ), ALU.subtract).then_inc(S.sub, 1)


def values_and_inverse_dve(nc, dve, S, i, pv, st):
    pv = pv.rearrange("p (m j) -> p m j", j=VB)
    dve.wait_ge(S.pv, at(i, 1, 1))
    nc.vector.reciprocal(st[:, 1, :].rearrange("p (m h) -> p m h", h=2), pv[:, :, 2 * DS:VB]).then_inc(S.inv, 1)
    dve.wait_ge(S.inv, at(i, 1, 1))
    return pv[:, :, 0:2 * DS].rearrange("p m (h d) -> p m h d", d=DS), over(st[:, 1, :].rearrange("p (m h) -> p m h", h=2), DS)


def self_attentions(nc, T, psum, dram):
    psT, psK, psS, psO, psM = psum
    with ExitStack() as ctx:
        def sb(name, shape, dt=F32):
            return ctx.enter_context(nc.sbuf_tensor(f"s_{name}", shape, dt))

        wout, bout = sb("wout", [P, WC, DIM]), sb("bout", [P, DIM])
        wgate, wgT = sb("wgate", [HS, DIM]), sb("wgT", [P, WC, HS])
        wqkv, wT = sb("wqkv", [P, 3 * WC, DIM]), sb("wT", [P, WC, 3 * DIM])
        am, sc = sb("am", [P, 3]), sb("sc", [P, 4, 3])
        mask8, mask2 = sb("mask8", [P, HH]), sb("mask2", [P, 2])
        sel, selb = sb("sel", [P, 2, 2, SQ]), sb("selb", [P, 2, 2, SQ], BF16)
        maskc, maskb = sb("maskc", [SQ, SQ]), sb("maskb", [SQ, SQ], BF16)
        iota_i, iota = sb("iota_i", [P, HS], I32), sb("iota", [P, HS])
        u, e, r8 = sb("u", [P, 3 * DIM]), sb("e", [P, 3 * DIM]), sb("r8", [P, 3 * DIM], BF16)
        q8T, k8bd = sb("q8T", [P, NC, P], BF16), sb("k8bd", [P, NC, 2, HH, SQ], BF16)
        prob, pT = sb("prob", [P, HS * SQ]), sb("pT", [P, HS // 2, P])
        prob2, pT2 = sb("prob2", [P, HS * SQ]), sb("pT2", [P, HS // 2, P])
        vbd, vbd2 = sb("vbd", [P, 2, HS // 2, VB]), sb("vbd2", [P, 2, VB])
        st, st2, o, oT = sb("st", [P, 2, HS]), sb("st2", [P, 2, HS]), sb("o", [P, DIM]), sb("oT", [P, WC, P])
        stats, mv, lx = sb("stats", [P, 6]), sb("mv", [P, 2]), sb("lx", [P, 5, 1])
        xn, xT = sb("xn", [P, WC, P]), sb("xT", [P, WC, P])
        gt, gs = sb("gt", [P, 5, HS]), sb("gs", [P, 4])
        q2, q2T = sb("q2", [P, DIM]), sb("q2T", [P, NC, P])
        kw, vw, ks = sb("kw", [P, DIM]), sb("vw", [P, DIM]), sb("ks", [P, 3, DS])
        krep, k2bd = sb("krep", [P, HH, DS]), sb("k2bd", [P, 2, HH, SQ])
        y = sb("y", [P, DIM])
        W, A, AS, G, GS, L = primed(nc, ctx, ("ws", "wout bout wgate wqkv gT gTe wT wTe m8 m2 sel causal maskb iota iotaf xb selb am amall sc stored passed"),
                                    ("att", ATT_SEMS), ("attsm", SM_SEMS), ("ffn", FFN_SEMS), ("ffnsm", SM_SEMS), ("ffnln", ROOT))
        stored = W.stored
        bf = psT[:, :].bitcast(BF16)
        att_scores, att_pv, att_proj = psS[:, :, :], psO[:, 0, 0:HS // 2 * VB], psM[:, 0:DIM]
        ffn_scores, ffn_pv = psK[:, :, :], psO[:, 1, 0:HS // 2 * VB]
        ffn_lnT, ffn_gate, ffn_T, ffn_dup = psT[:, 0:DIM], psT[:, DIM:DIM + HS], psT[:, 0:(NC + 1) * P], psO[:, 0, BANK - 2 * DS:BANK]
        block = ctx.enter_context(nc.Block())

        def latents(i):
            n = slice(i, i + 1) if isinstance(i, int) else bass.ds(i, 1)
            return T.xs[:, n, :].rearrange("p n c -> p (n c)")

        def pipeline(eng, step):
            step(None, None, None, 0)
            step(0, None, None, 1)
            step(1, 0, None, 2)
            with eng.Fori(0, NPAIR - 3) as i:
                step(i + 2, i + 1, i, i + 3)
            step(NPAIR - 1, NPAIR - 2, NPAIR - 3, None)
            step(None, NPAIR - 1, NPAIR - 2, None)
            step(None, None, NPAIR - 1, None)

        @block.sync
        def _(sp):
            sp.dma_start(wqkv[:, :, :], dram["L0_ffn_W_qkv"].rearrange("(k p) n -> p k n", p=P)).then_inc(W.wqkv, 16)
            sp.dma_start(wgate[:, :], dram["L0_ffn_W_gate"]).then_inc(W.wgate, 16)
            sp.dma_start(wout[:, :, :], dram["L0_attn_W_out"].rearrange("(k p) n -> p k n", p=P)).then_inc(W.wout, 16)
            sp.dma_start(bout[:, :], dram["L0_attn_b_out"].rearrange("(a n) -> a n", a=1).broadcast_to([P, DIM])).then_inc(W.bout, 16)
            out = dram["out"].rearrange("b q c -> (b q) c").rearrange("(n p) c -> n p c", p=P)
            with sp.Fori(0, NPAIR) as i:
                sp.wait_ge(G.y, at(i, 2, 2))
                sp.dma_start(out[bass.ds(i, 1), :, :].rearrange("n p c -> (n p) c"), y[:, :]).then_inc(stored, 16)
                sp.wait_ge(stored, 16 * i + 16)
                alone(sp, W.passed)

        @block.gpsimd
        def _(pool):
            for m, width, sem in ((mask8, DS, W.m8), (mask2, SQ, W.m2)):
                n = P // width
                nc.gpsimd.memset(m[:, :], 1.0).then_inc(sem, 1)
                pool.wait_ge(sem, 1)
                nc.gpsimd.affine_select(out=m[:, :], in_=m[:, :], compare_op=ALU.is_ge, fill=0.0, base=0,
                                        pattern=[[-width, n]], channel_multiplier=1).then_inc(sem, 1)
                pool.wait_ge(sem, 2)
                nc.gpsimd.affine_select(out=m[:, :], in_=m[:, :], compare_op=ALU.is_ge, fill=0.0, base=width - 1,
                                        pattern=[[width, n]], channel_multiplier=-1).then_inc(sem, 1)
            nc.gpsimd.memset(sel[:, :, :, :], 0.0).then_inc(W.sel, 1)
            pool.wait_ge(W.sel, 1)
            nc.gpsimd.affine_select(out=sel[:, :, :, :], in_=sel[:, :, :, :], compare_op=ALU.not_equal, fill=1.0, base=0,
                                    pattern=[[-SQ, 2], [0, 2], [-1, SQ]], channel_multiplier=1).then_inc(W.sel, 1)
            nc.gpsimd.memset(maskc[:, :], 0.0).then_inc(W.causal, 1)
            pool.wait_ge(W.causal, 1)
            nc.gpsimd.affine_select(out=maskc[:, :], in_=maskc[:, :], compare_op=ALU.is_ge, fill=-FAR, base=0,
                                    pattern=[[-1, SQ]], channel_multiplier=1).then_inc(W.causal, 1)
            nc.gpsimd.iota(iota_i[:, :], pattern=[[1, HS]], base=-HS, channel_multiplier=0).then_inc(W.iota, 1)
            pool.wait_ge(W.am, 1)
            nc.gpsimd.partition_all_reduce(sc[:, 0, :], am[:, :], P, ABSMAX).then_inc(W.amall, 1)
            pool.wait_ge(W.bout, 16)
            nc.gpsimd.tensor_tensor(T.xs[:, :, :], T.xs[:, :, :], bout[:, :].unsqueeze(1).broadcast_to([P, NPAIR, DIM]), ALU.add).then_inc(W.xb, 1)

        @block.tensor
        def _(pe):
            pe.wait_ge(W.wgate, 16)
            for k in range(WC):
                last = nc.tensor.transpose(psT[:, k * HS:(k + 1) * HS], wgate[:, k * P:(k + 1) * P], T.ident[0:HS, 0:HS])
            last.then_inc(W.gT, 1)
            pe.wait_ge(W.wqkv, 16)
            for k in range(WC):
                for f in range(3 * WC):
                    bank, n = (psK, psS)[k], f
                    last = nc.tensor.transpose(bank[:, n // 4, n % 4 * P:(n % 4 + 1) * P], wqkv[:, f, k * P:(k + 1) * P], T.ident[:, :])
                last.then_inc(W.wT, 1)
            pe.wait_ge(W.gTe, 1)
            pe.wait_ge(W.wTe, 2 * WC)
            pe.wait_ge(W.wout, 16)
            pe.wait_ge(W.selb, 1)
            pe.wait_ge(W.maskb, 1)

            def step(a, f, g, z):
                if a is not None:
                    pe.wait_ge(A.q8, at(a, 1, 1))
                    for n in range(2 * NC):
                        last = nc.tensor.transpose(bf[:, n * P:(n + 1) * P], r8[:, n * P:(n + 1) * P], T.identb[:, :])
                    last.then_inc(A.T, 1)
                    pe.wait_ge(A.x3, at(a, 1, 0))
                    for b in range(2):
                        last = nc.tensor.matmul(psM[:, b * DIM:(b + 1) * DIM], selb[:, b, :, :].rearrange("p c k -> p (c k)"),
                                                r8[:, 2 * DIM:3 * DIM], start=True, stop=True)
                    last.then_inc(A.dup, 1)
                if g is not None:
                    transpose_pe(nc, pe, T, GS, g, ffn_scores, prob2)
                if a is not None:
                    pe.wait_ge(A.qT, at(a, 1, 1))
                    pe.wait_ge(A.kbd, at(a, NC, NC))
                    scores_pe(nc, pe, AS, att_scores, q8T, lambda c, b: k8bd[:, c, b, :, :].rearrange("p h k -> p (h k)"))
                if f is not None:
                    pe.wait_ge(G.centred, at(f, 1, 1))
                    pe.wait_ge(A.oTe, at(f, 1, 1))
                    for k in range(WC):
                        last = nc.tensor.transpose(ffn_lnT[:, k * P:(k + 1) * P], xn[:, k, :], T.ident[:, :])
                    last.then_inc(G.lnT, 1)
                    pe.wait_ge(G.lnTe, at(f, 1, 1))
                    product(ffn_gate, lambda k: wgT[:, k, :])
                if f is not None:
                    if g is not None:
                        pe.wait_ge(GS.pTe, at(g, NC, NC))
                    product(psK[:, 0, :], lambda k: wT[:, k, 0:2 * DIM])
                    product(psK[:, 1, 0:DIM], lambda k: wT[:, k, 2 * DIM:3 * DIM])
                if a is not None:
                    transpose_pe(nc, pe, T, AS, a, att_scores, prob)
                if g is not None:
                    pe.wait_ge(G.y, at(g, 2, -1))
                    weigh_pe(nc, pe, GS, g, ffn_pv, pT2, lambda b, m: vbd2[:, b, :])
                if f is not None:
                    pe.wait_ge(G.krep, at(f, 1, 1))
                    nc.tensor.transpose(ffn_T[:, NC * P:(NC + 1) * P], krep[:, :, :].rearrange("p h d -> p (h d)"), T.ident[:, :])
                    pe.wait_ge(G.q, at(f, 1, 1))
                    for n in range(NC):
                        last = nc.tensor.transpose(ffn_T[:, n * P:(n + 1) * P], q2[:, n * P:(n + 1) * P], T.ident[:, :])
                    last.then_inc(G.T, 1)
                    pe.wait_ge(G.vtop, at(f, 1, 1))
                    for b in range(2):
                        last = nc.tensor.matmul(ffn_dup[:, b * DS:(b + 1) * DS], sel[:, b, :, :].rearrange("p c k -> p (c k)"),
                                                ks[:, 2, :], start=True, stop=True)
                    last.then_inc(G.dup, 1)
                    for b in range(2):
                        for c in range(NC):
                            nc.tensor.matmul(ffn_scores[b * SQ:(b + 1) * SQ, c, :], T.identb[0:SQ, 0:SQ],
                                             maskb[:, :].unsqueeze(1).broadcast_to([SQ, HH, SQ]), start=True, stop=False)
                if f is not None:
                    pe.wait_ge(G.qT, at(f, 1, 1))
                    pe.wait_ge(G.kbd, at(f, 1, 1))
                    scores_pe(nc, pe, GS, ffn_scores, q2T, lambda c, b: k2bd[:, b, :, :].rearrange("p h k -> p (h k)"), False)
                if a is not None:
                    pe.wait_ge(GS.vbd, at(a, 1, 0))
                    weigh_pe(nc, pe, AS, a, att_pv, pT, lambda b, m: vbd[:, b, m, :])
                    pe.wait_ge(A.o, at(a, 1, 1))
                    for k in range(WC):
                        last = nc.tensor.transpose(psT[:, k * P:(k + 1) * P], o[:, k * P:(k + 1) * P], T.ident[:, :])
                    last.then_inc(A.oT, 1)
                    pe.wait_ge(A.oTe, at(a, 1, 1))
                    for k in range(WC):
                        last = nc.tensor.matmul(att_proj, oT[:, k, :], wout[:, k, :], start=(k == 0), stop=(k == WC - 1))
                    last.then_inc(A.proj, 1)

            def product(out, w):
                for k in range(WC):
                    last = nc.tensor.matmul(out, xT[:, k, :], w(k), start=(k == 0), stop=(k == WC - 1))
                last.then_inc(G.mm, 1)

            pipeline(pe, step)

        @block.scalar
        def _(act):
            act.wait_ge(W.gT, 1)
            nc.scalar.activation(wgT[:, :, :], psT[:, 0:WC * HS].rearrange("p (k h) -> p k h", k=WC), ACT.Copy).then_inc(W.gTe, 1)
            for k in range(WC):
                act.wait_ge(W.wT, k + 1)
                bank = (psK, psS)[k]
                nc.scalar.activation(wT[:, k, 0:BANK], bank[:, 0, :], ACT.Copy).then_inc(W.wTe, 1)
                nc.scalar.activation(wT[:, k, BANK:3 * DIM], bank[:, 1, 0:3 * DIM - BANK], ACT.Copy).then_inc(W.wTe, 1)
            nc.scalar.preload_act_table_set(LN_EXP)
            act.wait_ge(W.sc, 5)

            def step(a, f, g, z):
                if a is not None:
                    act.wait_ge(A.T, at(a, 1, 1))
                    nc.scalar.activation(q8T[:, :, :].rearrange("p c n -> p (c n)"), bf[:, 0:NC * P], ACT.Copy).then_inc(A.qT, 1)
                if g is not None:
                    transposed_act(nc, act, GS, g, pT2, ffn_scores)
                if f is not None:
                    inverse_root_guess(nc, act, L, f, lx[:, 1, :], lx[:, 2, :], lx[:, 0, :])
                    act.wait_ge(G.lnT, at(f, 1, 1))
                    nc.scalar.activation(xT[:, :, :].rearrange("p k n -> p (k n)"), ffn_lnT, ACT.Copy).then_inc(G.lnTe, 1)
                if f is not None:
                    act.wait_ge(G.gsub, at(f, 1, 1))
                    nc.scalar.activation(gt[:, 4, :], gt[:, 3, :], ACT.Exp).then_inc(G.gexp, 1)
                if a is not None:
                    act.wait_ge(AS.sub, at(a, 1, 1))
                    nc.scalar.activation(prob[:, :], prob[:, :], ACT.Exp, scale=sc[:, 3, 0:1]).then_inc(AS.exp, 1)
                if f is not None:
                    act.wait_ge(G.mm, at(f, 3, 2))
                    nc.scalar.activation(q2[:, :], psK[:, 0, 0:DIM], ACT.Copy).then_inc(G.q, 1)
                    act.wait_ge(G.T, at(f, 1, 1))
                    nc.scalar.activation(q2T[:, :, :].rearrange("p k n -> p (k n)"), ffn_T[:, 0:DIM], ACT.Copy).then_inc(G.qT, 1)
                if a is not None:
                    transposed_act(nc, act, AS, a, pT, att_scores)
                if z is not None:
                    act.wait_ge(A.q8, at(z, 1, 0))
                    n = slice(z, z + 1) if isinstance(z, int) else bass.ds(z, 1)
                    for part in range(3):
                        cols = slice(part * DIM, (part + 1) * DIM)
                        last = nc.scalar.activation(u[:, cols], T.qkv[:, n, cols].rearrange("p n m -> p (n m)"), ACT.Copy, scale=sc[:, 2, part:part + 1])
                    last.then_inc(A.u, 1)
                if a is not None:
                    act.wait_ge(A.oT, at(a, 1, 1))
                    nc.scalar.activation(oT[:, :, :].rearrange("p k n -> p (k n)"), psT[:, 0:DIM], ACT.Copy).then_inc(A.oTe, 1)
                if f is not None:
                    act.wait_ge(GS.sub, at(f, 1, 1))
                    nc.scalar.activation(prob2[:, :], prob2[:, :], ACT.Exp, scale=1.0 / np.sqrt(DS)).then_inc(GS.exp, 1)

            pipeline(act, step)

        @block.vector
        def _(dve):
            nc.vector.tensor_reduce(am[:, :], T.amax[:, :, :].rearrange("p n g -> p g n"), AX.X, ALU.max).then_inc(W.am, 1)
            dve.wait_ge(W.sel, 2)
            nc.vector.tensor_copy(selb[:, :, :, :], sel[:, :, :, :]).then_inc(W.selb, 1)
            dve.wait_ge(W.iota, 1)
            nc.vector.tensor_copy(iota[:, :], iota_i[:, :]).then_inc(W.iotaf, 1)
            dve.wait_ge(W.amall, 1)
            nc.vector.tensor_scalar(sc[:, 1, :], sc[:, 0, :], 1.0 / FP8_MAX, None, ALU.mult).then_inc(W.sc, 1)
            dve.wait_ge(W.sc, 1)
            nc.vector.reciprocal(sc[:, 2, :], sc[:, 1, :]).then_inc(W.sc, 1)
            nc.vector.tensor_tensor(sc[:, 3, 1:2], sc[:, 1, 0:1], sc[:, 1, 1:2], ALU.mult).then_inc(W.sc, 1)
            dve.wait_ge(W.sc, 3)
            nc.vector.tensor_scalar(sc[:, 3, 0:1], sc[:, 3, 1:2], float(1.0 / np.sqrt(DS)), None, ALU.mult).then_inc(W.sc, 1)
            dve.wait_ge(W.sc, 4)
            nc.vector.tensor_copy(sc[:, 3, 2:3], sc[:, 1, 2:3]).then_inc(W.sc, 1)
            dve.wait_ge(W.m8, 3)
            dve.wait_ge(W.m2, 3)
            dve.wait_ge(W.causal, 2)
            nc.vector.tensor_copy(maskb[:, :], maskc[:, :]).then_inc(W.maskb, 1)
            for b in range(2):
                nc.vector.tensor_copy(vbd2[:, b, 2 * DS:VB], mask2[:, :])
                nc.vector.tensor_copy(vbd[:, b, :, 2 * DS:VB], mask2[:, :].unsqueeze(1).broadcast_to([P, HS // 2, 2]))
            dve.wait_ge(W.iotaf, 1)
            dve.wait_ge(W.sc, 5)

            def step(a, f, g, z):
                if f is not None:
                    nc.vector.bn_stats(stats[:, :], latents(f)).then_inc(G.stats, 1)
                if a is not None:
                    dve.wait_ge(A.qT, at(a, 1, 1))
                    block_diagonal(a, 0)
                if f is not None:
                    dve.wait_ge(G.stats, at(f, 1, 1))
                    alone(dve, W.passed)
                    nc.vector.bn_aggr(mv[:, :], stats[:, :]).then_inc(G.moments, 1)
                    dve.wait_ge(G.moments, at(f, 1, 1))
                    inverse_root_start(nc, dve, L.x, lx[:, 0, :], mv[:, 1:2], 1)
                if a is not None:
                    block_diagonal(a, 1)
                if f is not None:
                    inverse_root_end(nc, dve, L, f, lx[:, 2, :], lx[:, 3, :], lx[:, 0, :], lx[:, 4, :])
                    dve.wait_ge(L.root, at(f, 1, 1))
                    nc.vector.tensor_scalar(xn[:, :, :].rearrange("p k n -> p (k n)"), latents(f), mv[:, 0:1], lx[:, 4, :],
                                            ALU.subtract, ALU.mult).then_inc(G.centred, 1)
                if a is not None:
                    dve.wait_ge(A.dup, at(a, 1, 1))
                    for b in range(2):
                        last = nc.vector.tensor_tensor(vbd[:, b, :, 0:2 * DS].rearrange("p m (h d) -> p m h d", d=DS),
                                                       psM[:, b * DIM:(b + 1) * DIM].rearrange("p (m h d) -> p m h d", h=2, d=DS),
                                                       mask2[:, :].unsqueeze(1).unsqueeze(3).broadcast_to([P, HS // 2, 2, DS]), ALU.mult)
                    last.then_inc(AS.vbd, 1)
                    softmax_dve(nc, dve, AS, a, att_scores.rearrange("p a n -> p (a n)"), prob[:, :], st)
                if f is not None:
                    select_head(f)
                    selected(f)
                if f is not None:
                    dve.wait_ge(G.qT, at(f, 1, 1))
                    k2 = ffn_T[:, NC * P:(NC + 1) * P].rearrange("p (b k) -> p b k", b=2).unsqueeze(2).broadcast_to([P, 2, HH, SQ])
                    nc.vector.tensor_tensor(k2bd[:, :, :, :], k2, mask8[:, :].unsqueeze(1).unsqueeze(3).broadcast_to([P, 2, HH, SQ]), ALU.mult).then_inc(G.kbd, 1)
                if g is not None:
                    pv, inv = values_and_inverse_dve(nc, dve, GS, g, ffn_pv, st2)
                    dve.wait_ge(stored, 16 * g)
                    nc.vector.tensor_tensor(y[:, :].rearrange("p (m h d) -> p m h d", h=2, d=DS), pv, inv, ALU.mult).then_inc(G.y, 1)
                    dve.wait_ge(G.y, at(g, 2, 1))
                    nc.vector.tensor_tensor(y[:, :], y[:, :], latents(g), ALU.add).then_inc(G.y, 1)
                if f is not None:
                    dve.wait_ge(G.dup, at(f, 1, 1))
                    nc.vector.tensor_tensor(vbd2[:, :, 0:2 * DS].rearrange("p b (h d) -> p b h d", d=DS),
                                            ffn_dup.rearrange("p (b d) -> p b d", b=2).unsqueeze(2).broadcast_to([P, 2, 2, DS]),
                                            mask2[:, :].unsqueeze(1).unsqueeze(3).broadcast_to([P, 2, 2, DS]), ALU.mult).then_inc(GS.vbd, 1)
                if z is not None:
                    quantise(z)
                if a is not None:
                    pv, inv = values_and_inverse_dve(nc, dve, AS, a, att_pv, st)
                    nc.vector.scalar_tensor_tensor(o[:, :].rearrange("p (m h d) -> p m h d", h=2, d=DS), pv, sc[:, 1, 2:3], inv,
                                                   ALU.mult, ALU.mult).then_inc(A.o, 1)
                if f is not None:
                    softmax_dve(nc, dve, GS, f, ffn_scores.rearrange("p a n -> p (a n)"), prob2[:, :], st2)
                if a is not None:
                    if f is None:
                        dve.wait_ge(W.xb, 1)
                    dve.wait_ge(A.proj, at(a, 1, 1))
                    nc.vector.tensor_tensor(latents(a), att_proj, latents(a), ALU.add).then_inc(A.x3, 1)
                if a is not None:
                    dve.wait_ge(A.x3, at(a, 1, 1))

            def quantise(z):
                dve.wait_ge(A.u, at(z, 1, 1))
                nc.vector.tensor_scalar(e[:, :].bitcast(I32), u[:, :].bitcast(I32), 0x7F800000, None, ALU.bitwise_and).then_inc(A.expo, 1)
                dve.wait_ge(A.expo, at(z, 1, 1))
                nc.vector.tensor_scalar(e[:, :], e[:, :], 2.0 ** -6, 1.5 * 2.0 ** 20, ALU.max, ALU.mult).then_inc(A.magic, 1)
                dve.wait_ge(A.magic, at(z, 1, 1))
                nc.vector.tensor_tensor(u[:, :], u[:, :], e[:, :], ALU.add).then_inc(A.sum, 1)
                dve.wait_ge(A.sum, at(z, 1, 1))
                nc.vector.tensor_tensor(r8[:, :], u[:, :], e[:, :], ALU.subtract).then_inc(A.q8, 1)

            def block_diagonal(a, c):
                k8 = bf[:, (NC + c) * P:(NC + c + 1) * P].rearrange("p (b k) -> p b k", b=2).unsqueeze(2).broadcast_to([P, 2, HH, SQ])
                m8 = mask8[:, :].unsqueeze(1).unsqueeze(3).broadcast_to([P, 2, HH, SQ])
                nc.vector.tensor_tensor(k8bd[:, c, :, :, :], k8, m8, ALU.mult).then_inc(A.kbd, 1)

            def select_head(f):
                dve.wait_ge(G.mm, at(f, 3, 1))
                nc.vector.tensor_reduce(gs[:, 0:1], ffn_gate, AX.X, ALU.max).then_inc(G.gmax, 1)
                dve.wait_ge(G.gmax, at(f, 1, 1))
                nc.vector.tensor_scalar(gt[:, 3, :], ffn_gate, gs[:, 0:1], None, ALU.subtract).then_inc(G.gsub, 1)
                nc.vector.tensor_scalar(gt[:, 0, :], ffn_gate, gs[:, 0:1], None, ALU.is_ge).then_inc(G.eq, 1)
                dve.wait_ge(G.eq, at(f, 1, 1))
                nc.vector.tensor_tensor(gt[:, 1, :], gt[:, 0, :], iota[:, :], ALU.mult).then_inc(G.cand, 1)
                dve.wait_ge(G.cand, at(f, 1, 1))
                nc.vector.tensor_reduce(gs[:, 1:2], gt[:, 1, :], AX.X, ALU.min).then_inc(G.first, 1)
                dve.wait_ge(G.first, at(f, 1, 1))
                nc.vector.tensor_scalar(gt[:, 2, :], iota[:, :], gs[:, 1:2], None, ALU.is_equal).then_inc(G.ind, 1)
                dve.wait_ge(G.gexp, at(f, 1, 1))
                nc.vector.tensor_reduce(gs[:, 2:3], gt[:, 4, :], AX.X, ALU.add).then_inc(G.gsum, 1)
                dve.wait_ge(G.gsum, at(f, 1, 1))
                nc.vector.reciprocal(gs[:, 3:4], gs[:, 2:3]).then_inc(G.gtop, 1)

            def selected(f):
                dve.wait_ge(G.ind, at(f, 1, 1))
                dve.wait_ge(G.q, at(f, 1, 1))
                nc.vector.tensor_tensor(kw[:, :].rearrange("p (h d) -> p h d", d=DS), psK[:, 0, DIM:2 * DIM].rearrange("p (h d) -> p h d", d=DS),
                                        over(gt[:, 2, :], DS), ALU.mult).then_inc(G.kw, 1)
                dve.wait_ge(G.mm, at(f, 3, 3))
                nc.vector.tensor_tensor(vw[:, :].rearrange("p (h d) -> p h d", d=DS), psK[:, 1, 0:DIM].rearrange("p (h d) -> p h d", d=DS),
                                        over(gt[:, 2, :], DS), ALU.mult).then_inc(G.vw, 1)
                dve.wait_ge(G.kw, at(f, 1, 1))
                nc.vector.tensor_reduce(ks[:, 0, :], kw[:, :].rearrange("p (h d) -> p d h", d=DS), AX.X, ALU.add).then_inc(G.ks, 1)
                dve.wait_ge(G.vw, at(f, 1, 1))
                nc.vector.tensor_reduce(ks[:, 1, :], vw[:, :].rearrange("p (h d) -> p d h", d=DS), AX.X, ALU.add).then_inc(G.vs, 1)
                dve.wait_ge(G.ks, at(f, 1, 1))
                nc.vector.tensor_copy(krep[:, :, :], ks[:, 0, :].unsqueeze(1).broadcast_to([P, HH, DS])).then_inc(G.krep, 1)
                dve.wait_ge(G.gtop, at(f, 1, 1))
                dve.wait_ge(G.vs, at(f, 1, 1))
                nc.vector.tensor_scalar(ks[:, 2, :], ks[:, 1, :], gs[:, 3:4], None, ALU.mult).then_inc(G.vtop, 1)

            pipeline(dve, step)


def build(nc, dram):
    with ExitStack() as ctx:
        def sb(name, shape, dt=F32):
            return ctx.enter_context(nc.sbuf_tensor(name, shape, dt))

        def pb(name, banks):
            return ctx.enter_context(nc.psum_tensor(name, [P, banks, BANK] if banks > 1 else [P, BANK], F32))

        psum = pb("psT", 1), pb("psK", 2), pb("psS", 2), pb("psO", 2), pb("psM", 1)
        T = Shared()
        T.ident, T.identb = sb("ident", [P, P]), sb("identb", [P, P], BF16)
        T.ones, T.zero, T.shift, T.gcol = sb("ones", [P, P]), sb("zero", [P, 1]), sb("shift", [P, 1]), sb("gcol", [P, 2])
        T.xs, T.amax = sb("xs", [P, NPAIR, DIM]), sb("amax", [P, NPAIR, 3])
        with ExitStack() as crossing:
            T.big = crossing.enter_context(nc.sbuf_tensor("big", [P, NPAIR * 2 * HQ], F32))
            T.queries = T.big[:, :].rearrange("p (n b h q) -> p n b h q", n=NPAIR, b=2, q=SQ)
            with ExitStack() as keys:
                T.wkh = keys.enter_context(nc.sbuf_tensor("wkh", [P, INNER], F32R))
                T.wkl = keys.enter_context(nc.sbuf_tensor("wkl", [P, INNER], F32R))
                queries(nc, T, psum, dram)
                cross_attention(nc, T, psum, dram)
            T.qkv = crossing.enter_context(nc.sbuf_tensor("qkv", [P, NPAIR, 3 * DIM], F32))
            project(nc, T, psum, dram)
            self_attentions(nc, T, psum, dram)


_INS = ["x", "ctx_1024", "L0_xattn_Wq", "L0_xattn_Wk", "L0_xattn_Wv", "L0_xattn_Wo", "L0_xattn_gq", "L0_xattn_gk",
        "L0_attn_W_qkv", "L0_attn_W_out", "L0_attn_b_out", "L0_ffn_W_gate", "L0_ffn_W_qkv"]


def kernel(**inputs):
    import concourse.bacc as bacc
    from concourse.bass_utils import run_bass_kernel_spmd

    nc = bacc.Bacc("TRN2", target_bir_lowering=False, num_devices=1)
    arrays, dram = {}, {}
    for name in _INS:
        a = np.ascontiguousarray(inputs[name])
        arrays[f"in_{name}"] = a
        dram[name] = nc.dram_tensor(f"in_{name}", a.shape, mybir.dt.from_np(a.dtype), kind="ExternalInput").ap()
    dram["out"] = nc.dram_tensor("out", (B, SQ, DIM), F32, kind="ExternalOutput").ap()
    build(nc, dram)
    result = run_bass_kernel_spmd(nc, [arrays], core_ids=[0])
    return result.results[0]["out"]
```
